# Optimizing a Trainium2 kernel written in Bass

```python
import numpy as np
import jax
import jax.numpy as jnp

def _softmax(x, axis=-1):
    return jax.nn.softmax(x, axis=axis)

def _gelu(x):
    return jax.nn.gelu(x, approximate=True)

def _silu(x):
    return jax.nn.silu(x)

def _sigmoid(x):
    return jax.nn.sigmoid(x)

def _layernorm(x, axis=-1, eps=1e-05):
    m = jnp.mean(x, axis=axis, keepdims=True)
    v = jnp.var(x, axis=axis, keepdims=True)
    return (x - m) / jnp.sqrt(v + eps)

def _scatter_add(tgt, idx, src, axis=0):
    return tgt.at[idx].add(src)

def _segment_sum(src, seg, n):
    return jax.ops.segment_sum(src, seg, n)
kernel_name = 'mk_macaron_d2_jaxref_r8_38258b'

def setup_inputs(seed: int=0):
    np.random.seed(seed)
    _w = jnp.asarray

    def _L0_attn_setup():
        import jax, jax.numpy as jnp
        import numpy as np
        D_MODEL = 128
        D_STATE = 64
        HEADDIM = 64
        D_INNER = 2 * D_MODEL
        NHEADS = D_INNER // HEADDIM
        D_IN_PROJ = 2 * D_INNER + 2 * D_STATE + NHEADS
        CHANNELS = D_INNER + 2 * D_STATE
        KSIZE = 4
        LN_EPS = 1e-05

        def _segsum(x):
            T = x.shape[-1]
            cs = jnp.cumsum(x, axis=-1)
            seg = cs[..., :, None] - cs[..., None, :]
            mask = jnp.tril(jnp.ones((T, T), bool))
            return jnp.where(mask, seg, -jnp.inf)

        def _ssd(X, A, B, C, block_len):
            b, Lseq, h, p = X.shape
            c = Lseq // block_len
            X = X.reshape(b, c, block_len, h, p)
            A = A.reshape(b, c, block_len, h).transpose(0, 3, 1, 2)
            B = B.reshape(b, c, block_len, -1)
            C = C.reshape(b, c, block_len, -1)
            A_cumsum = jnp.cumsum(A, axis=-1)
            Lmat = jnp.exp(_segsum(A))
            Y_diag = jnp.einsum('bcln,bcsn,bhcls,bcshp->bclhp', C, B, Lmat, X)
            decay_states = jnp.exp(A_cumsum[..., -1:] - A_cumsum)
            states = jnp.einsum('bcln,bhcl,bclhp->bchpn', B, decay_states, X)
            init = jnp.zeros_like(states[:, :1])
            states = jnp.concatenate([init, states], axis=1)
            A_last = jnp.pad(A_cumsum[..., -1], ((0, 0), (0, 0), (1, 0)))
            decay_chunk = jnp.exp(_segsum(A_last))
            new_states = jnp.einsum('bhzc,bchpn->bzhpn', decay_chunk, states)
            states_off, final_state = (new_states[:, :-1], new_states[:, -1])
            state_decay_out = jnp.exp(A_cumsum)
            Y_off = jnp.einsum('bcln,bchpn,bhcl->bclhp', C, states_off, state_decay_out)
            Y = (Y_diag + Y_off).reshape(b, Lseq, h, p)
            return (Y, final_state)
        key = jax.random.key(seed)
        ks = jax.random.split(key, 8)
        B, L = (2, 256)
        u = jax.random.normal(ks[0], (B, L, D_MODEL), jnp.float32)
        W_in1 = jax.random.normal(ks[1], (D_IN_PROJ, D_MODEL), jnp.float32) * 0.02
        A_log = jnp.log(jax.random.uniform(ks[2], (NHEADS,), jnp.float32, 1.0, 16.0))
        conv_w = jax.random.normal(ks[3], (CHANNELS, CHANNELS, KSIZE), jnp.float32) / np.sqrt(CHANNELS * KSIZE)
        conv_b = jax.random.normal(ks[4], (CHANNELS,), jnp.float32) * 0.01
        prelu_a = jnp.array(0.25, jnp.float32)
        W_in2 = jax.random.normal(ks[5], (D_INNER, D_MODEL), jnp.float32) * 0.02
        W_in3 = jax.random.normal(ks[6], (D_MODEL, D_INNER), jnp.float32) * 0.02
        ln_g = jnp.ones((D_INNER,), jnp.float32)
        ln_b = jnp.zeros((D_INNER,), jnp.float32)
        return {'u': u, 'W_in1': W_in1, 'A_log': A_log, 'conv_w': conv_w, 'conv_b': conv_b, 'prelu_a': prelu_a, 'W_in2': W_in2, 'W_in3': W_in3, 'ln_g': ln_g, 'ln_b': ln_b}
    _L0_attn_in = _L0_attn_setup()

    def _L0_ffn_setup():
        import jax, jax.numpy as jnp
        import numpy as np
        E = 16
        K = 2
        DIM = 128
        INTER = 88
        B, S = (4, 128)
        key = jax.random.key(seed)
        ks = jax.random.split(key, 5)
        x = jax.random.normal(ks[0], (B, S, DIM), dtype=jnp.float32)
        Wg = jax.random.normal(ks[1], (E, DIM), dtype=jnp.float32) * 0.02
        W1 = jax.random.normal(ks[2], (E, DIM, INTER), dtype=jnp.float32) * 0.02
        W3 = jax.random.normal(ks[3], (E, DIM, INTER), dtype=jnp.float32) * 0.02
        W2 = jax.random.normal(ks[4], (E, INTER, DIM), dtype=jnp.float32) * 0.02
        return {'x': x, 'Wg': Wg, 'W1': W1, 'W2': W2, 'W3': W3}
    _L0_ffn_in = _L0_ffn_setup()

    def _L1_attn_setup():
        import jax, jax.numpy as jnp
        import numpy as np
        import math
        D_MODEL = 128
        N_HEADS = 16
        HEAD_DIM = D_MODEL // N_HEADS

        def _apply_rope_full(x):
            B, S, D = x.shape
            half = D // 2
            pos = jnp.arange(S, dtype=jnp.float32)[:, None]
            freqs = 1.0 / 10000.0 ** (jnp.arange(half, dtype=jnp.float32) / half)
            ang = pos * freqs[None, :]
            sin, cos = (jnp.sin(ang), jnp.cos(ang))
            x1, x2 = (x[..., :half], x[..., half:])
            return jnp.concatenate([x1 * cos - x2 * sin, x1 * sin + x2 * cos], axis=-1)

        def _alibi_slopes(n_heads):
            return jnp.array([2.0 ** (-8.0 * (i + 1) / n_heads) for i in range(n_heads)], dtype=jnp.float32)
        key = jax.random.key(seed)
        ks = jax.random.split(key, 5)
        B, S, D = (2, 256, D_MODEL)
        scale = 1.0 / math.sqrt(D)
        return {'x': jax.random.normal(ks[0], (B, S, D), dtype=jnp.float32), 'wq': jax.random.normal(ks[1], (D, D), dtype=jnp.float32) * scale, 'wk': jax.random.normal(ks[2], (D, D), dtype=jnp.float32) * scale, 'wv': jax.random.normal(ks[3], (D, D), dtype=jnp.float32) * scale, 'out_w': jax.random.normal(ks[4], (D, D), dtype=jnp.float32) * scale, 'out_b': jnp.zeros((D,), dtype=jnp.float32)}
    _L1_attn_in = _L1_attn_setup()

    def _L1_ffn_setup():
        import jax, jax.numpy as jnp
        import numpy as np
        B, S, H, I, E_ROUTED, TOP_K = (8, 256, 128, 256, 8, 2)

        def _expert(x, Wg, Wu, Wd):
            return jax.nn.silu(x @ Wg.T) * (x @ Wu.T) @ Wd.T
        key = jax.random.key(seed)
        ks = jax.random.split(key, 9)
        s = 0.02
        return {'x': jax.random.normal(ks[0], (B, S, H), dtype=jnp.float32), 'Wg_s': jax.random.normal(ks[1], (I, H), dtype=jnp.float32) * s, 'Wu_s': jax.random.normal(ks[2], (I, H), dtype=jnp.float32) * s, 'Wd_s': jax.random.normal(ks[3], (H, I), dtype=jnp.float32) * s, 'Wg': jax.random.normal(ks[4], (E_ROUTED, I, H), dtype=jnp.float32) * s, 'Wu': jax.random.normal(ks[5], (E_ROUTED, I, H), dtype=jnp.float32) * s, 'Wd': jax.random.normal(ks[6], (E_ROUTED, H, I), dtype=jnp.float32) * s, 'Wr': jax.random.normal(ks[7], (E_ROUTED, H), dtype=jnp.float32) * s, 'rb': jnp.zeros((E_ROUTED,), dtype=jnp.float32)}
    _L1_ffn_in = _L1_ffn_setup()
    _d = {'L0_attn_u': _L0_attn_in['u'], 'L0_attn_W_in1': _L0_attn_in['W_in1'], 'L0_attn_A_log': _L0_attn_in['A_log'], 'L0_attn_conv_w': _L0_attn_in['conv_w'], 'L0_attn_conv_b': _L0_attn_in['conv_b'], 'L0_attn_prelu_a': _L0_attn_in['prelu_a'], 'L0_attn_W_in2': _L0_attn_in['W_in2'], 'L0_attn_W_in3': _L0_attn_in['W_in3'], 'L0_attn_ln_g': _L0_attn_in['ln_g'], 'L0_attn_ln_b': _L0_attn_in['ln_b'], 'L0_ffn_Wg': _L0_ffn_in['Wg'], 'L0_ffn_W1': _L0_ffn_in['W1'], 'L0_ffn_W2': _L0_ffn_in['W2'], 'L0_ffn_W3': _L0_ffn_in['W3'], 'L1_attn_wq': _L1_attn_in['wq'], 'L1_attn_wk': _L1_attn_in['wk'], 'L1_attn_wv': _L1_attn_in['wv'], 'L1_attn_out_w': _L1_attn_in['out_w'], 'L1_attn_out_b': _L1_attn_in['out_b'], 'L1_ffn_Wg_s': _L1_ffn_in['Wg_s'], 'L1_ffn_Wu_s': _L1_ffn_in['Wu_s'], 'L1_ffn_Wd_s': _L1_ffn_in['Wd_s'], 'L1_ffn_Wg': _L1_ffn_in['Wg'], 'L1_ffn_Wu': _L1_ffn_in['Wu'], 'L1_ffn_Wd': _L1_ffn_in['Wd'], 'L1_ffn_Wr': _L1_ffn_in['Wr'], 'L1_ffn_rb': _L1_ffn_in['rb']}
    _x0 = _d['L0_attn_u']
    _d['L0_attn_u'] = jax.random.normal(jax.random.fold_in(jax.random.key(seed), 1), (16, 256, 128), dtype=_x0.dtype)
    del _x0
    return _d

def reference(L0_attn_u, L0_attn_W_in1, L0_attn_A_log, L0_attn_conv_w, L0_attn_conv_b, L0_attn_prelu_a, L0_attn_W_in2, L0_attn_W_in3, L0_attn_ln_g, L0_attn_ln_b, L0_ffn_Wg, L0_ffn_W1, L0_ffn_W2, L0_ffn_W3, L1_attn_wq, L1_attn_wk, L1_attn_wv, L1_attn_out_w, L1_attn_out_b, L1_ffn_Wg_s, L1_ffn_Wu_s, L1_ffn_Wd_s, L1_ffn_Wg, L1_ffn_Wu, L1_ffn_Wd, L1_ffn_Wr, L1_ffn_rb):

    def _L0_attn_ref(u, W_in1, A_log, conv_w, conv_b, prelu_a, W_in2, W_in3, ln_g, ln_b):
        import jax, jax.numpy as jnp
        import numpy as np
        D_MODEL = 128
        D_STATE = 64
        HEADDIM = 64
        D_INNER = 2 * D_MODEL
        NHEADS = D_INNER // HEADDIM
        D_IN_PROJ = 2 * D_INNER + 2 * D_STATE + NHEADS
        CHANNELS = D_INNER + 2 * D_STATE
        KSIZE = 4
        LN_EPS = 1e-05

        def _segsum(x):
            T = x.shape[-1]
            cs = jnp.cumsum(x, axis=-1)
            seg = cs[..., :, None] - cs[..., None, :]
            mask = jnp.tril(jnp.ones((T, T), bool))
            return jnp.where(mask, seg, -jnp.inf)

        def _ssd(X, A, B, C, block_len):
            b, Lseq, h, p = X.shape
            c = Lseq // block_len
            X = X.reshape(b, c, block_len, h, p)
            A = A.reshape(b, c, block_len, h).transpose(0, 3, 1, 2)
            B = B.reshape(b, c, block_len, -1)
            C = C.reshape(b, c, block_len, -1)
            A_cumsum = jnp.cumsum(A, axis=-1)
            Lmat = jnp.exp(_segsum(A))
            Y_diag = jnp.einsum('bcln,bcsn,bhcls,bcshp->bclhp', C, B, Lmat, X)
            decay_states = jnp.exp(A_cumsum[..., -1:] - A_cumsum)
            states = jnp.einsum('bcln,bhcl,bclhp->bchpn', B, decay_states, X)
            init = jnp.zeros_like(states[:, :1])
            states = jnp.concatenate([init, states], axis=1)
            A_last = jnp.pad(A_cumsum[..., -1], ((0, 0), (0, 0), (1, 0)))
            decay_chunk = jnp.exp(_segsum(A_last))
            new_states = jnp.einsum('bhzc,bchpn->bzhpn', decay_chunk, states)
            states_off, final_state = (new_states[:, :-1], new_states[:, -1])
            state_decay_out = jnp.exp(A_cumsum)
            Y_off = jnp.einsum('bcln,bchpn,bhcl->bclhp', C, states_off, state_decay_out)
            Y = (Y_diag + Y_off).reshape(b, Lseq, h, p)
            return (Y, final_state)
        Bsz, L, _ = u.shape
        zxbcdt = u @ W_in1.T
        A = -jnp.exp(A_log)
        z = zxbcdt[..., :D_INNER]
        xBC = zxbcdt[..., D_INNER:D_INNER + CHANNELS]
        dt = zxbcdt[..., D_INNER + CHANNELS:]
        dt_safe = jnp.where(dt <= 20.0, dt, 0.0)
        dt = jnp.where(dt <= 20.0, jnp.log1p(jnp.exp(dt_safe)), dt)
        A_t = dt * A[None, None, :]
        xt = xBC.transpose(0, 2, 1)
        conv = jax.lax.conv_general_dilated(xt, conv_w, (1,), [(KSIZE - 1, 0)], dimension_numbers=('NCH', 'OIH', 'NCH'))
        conv = conv + conv_b[None, :, None]
        conv = jnp.maximum(conv, 0) + prelu_a * jnp.minimum(conv, 0)
        xBC_conv = conv.transpose(0, 2, 1)
        x = xBC_conv[..., :D_INNER].reshape(Bsz, L, NHEADS, HEADDIM)
        Bmat = xBC_conv[..., D_INNER:D_INNER + D_STATE]
        Cmat = xBC_conv[..., D_INNER + D_STATE:]
        Y, _ = _ssd(x, A_t, Bmat, Cmat, L // 4)
        out = Y.reshape(Bsz, L, D_INNER)
        u2 = jax.nn.gelu(u @ W_in2.T, approximate=False)
        h = u2 * out
        mu = jnp.mean(h, axis=-1, keepdims=True)
        var = jnp.mean((h - mu) ** 2, axis=-1, keepdims=True)
        hn = (h - mu) / jnp.sqrt(var + LN_EPS) * ln_g + ln_b
        return hn @ W_in3.T

    def _L0_ffn_ref(x, Wg, W1, W2, W3):
        import jax, jax.numpy as jnp
        import numpy as np
        E = 16
        K = 2
        DIM = 128
        INTER = 88
        B, S = (4, 128)
        Bb, Ss, D = x.shape
        xf = x.reshape(-1, D)
        logits = xf @ Wg.T
        probs = jax.nn.softmax(logits, axis=-1)
        topw, topi = jax.lax.top_k(probs, K)
        topw = topw / topw.sum(axis=-1, keepdims=True)
        gates = (jax.nn.one_hot(topi, E, dtype=xf.dtype) * topw[..., None]).sum(axis=1)
        out = jnp.zeros_like(xf)
        for e in range(E):
            h = jax.nn.silu(xf @ W1[e]) * (xf @ W3[e])
            out = out + gates[:, e:e + 1] * (h @ W2[e])
        return out.reshape(Bb, Ss, D)

    def _L1_attn_ref(x, wq, wk, wv, out_w, out_b):
        import jax, jax.numpy as jnp
        import numpy as np
        import math
        D_MODEL = 128
        N_HEADS = 16
        HEAD_DIM = D_MODEL // N_HEADS

        def _apply_rope_full(x):
            B, S, D = x.shape
            half = D // 2
            pos = jnp.arange(S, dtype=jnp.float32)[:, None]
            freqs = 1.0 / 10000.0 ** (jnp.arange(half, dtype=jnp.float32) / half)
            ang = pos * freqs[None, :]
            sin, cos = (jnp.sin(ang), jnp.cos(ang))
            x1, x2 = (x[..., :half], x[..., half:])
            return jnp.concatenate([x1 * cos - x2 * sin, x1 * sin + x2 * cos], axis=-1)

        def _alibi_slopes(n_heads):
            return jnp.array([2.0 ** (-8.0 * (i + 1) / n_heads) for i in range(n_heads)], dtype=jnp.float32)
        B, S, D = x.shape
        H, Dh = (N_HEADS, HEAD_DIM)
        q = x @ wq.T
        k = x @ wk.T
        v = x @ wv.T
        q = _apply_rope_full(q)
        k = _apply_rope_full(k)
        q = q.reshape(B, S, H, Dh).transpose(0, 2, 1, 3)
        k = k.reshape(B, S, H, Dh).transpose(0, 2, 1, 3)
        v = v.reshape(B, S, H, Dh).transpose(0, 2, 1, 3)
        scores = jnp.einsum('bhqd,bhkd->bhqk', q, k) / math.sqrt(Dh)
        pos = jnp.arange(S, dtype=jnp.float32)
        rel = pos[None, :] - pos[:, None]
        scores = scores + _alibi_slopes(H)[None, :, None, None] * rel[None, None]
        causal = jnp.triu(jnp.ones((S, S), dtype=bool), k=1)
        scores = jnp.where(causal[None, None], jnp.float32(-1000000000.0), scores)
        attn = jax.nn.softmax(scores, axis=-1)
        out = jnp.einsum('bhqk,bhkd->bhqd', attn, v)
        out = out.transpose(0, 2, 1, 3).reshape(B, S, D)
        return out @ out_w.T + out_b

    def _L1_ffn_ref(x, Wg_s, Wu_s, Wd_s, Wg, Wu, Wd, Wr, rb):
        import jax, jax.numpy as jnp
        import numpy as np
        B, S, H, I, E_ROUTED, TOP_K = (8, 256, 128, 256, 8, 2)

        def _expert(x, Wg, Wu, Wd):
            return jax.nn.silu(x @ Wg.T) * (x @ Wu.T) @ Wd.T
        shared = _expert(x, Wg_s, Wu_s, Wd_s)
        logits = jnp.einsum('bsh,eh->bse', x, Wr) + rb
        probs = jax.nn.sigmoid(logits)
        scores, idx = jax.lax.top_k(probs, TOP_K)
        cw = (jax.nn.one_hot(idx, E_ROUTED, dtype=x.dtype) * scores[..., None]).sum(-2)
        out = shared
        for e in range(E_ROUTED):
            out = out + cw[..., e:e + 1] * _expert(x, Wg[e], Wu[e], Wd[e])
        return out
    x = L0_attn_u
    x = x + 0.5 * _L0_ffn_ref(_layernorm(x, axis=-1), L0_ffn_Wg, L0_ffn_W1, L0_ffn_W2, L0_ffn_W3)
    x = x + _L0_attn_ref(_layernorm(x, axis=-1), L0_attn_W_in1, L0_attn_A_log, L0_attn_conv_w, L0_attn_conv_b, L0_attn_prelu_a, L0_attn_W_in2, L0_attn_W_in3, L0_attn_ln_g, L0_attn_ln_b)
    x = x + 0.5 * _L0_ffn_ref(_layernorm(x, axis=-1), L0_ffn_Wg, L0_ffn_W1, L0_ffn_W2, L0_ffn_W3)
    x = x + 0.5 * _L1_ffn_ref(_layernorm(x, axis=-1), L1_ffn_Wg_s, L1_ffn_Wu_s, L1_ffn_Wd_s, L1_ffn_Wg, L1_ffn_Wu, L1_ffn_Wd, L1_ffn_Wr, L1_ffn_rb)
    x = x + _L1_attn_ref(_layernorm(x, axis=-1), L1_attn_wq, L1_attn_wk, L1_attn_wv, L1_attn_out_w, L1_attn_out_b)
    x = x + 0.5 * _L1_ffn_ref(_layernorm(x, axis=-1), L1_ffn_Wg_s, L1_ffn_Wu_s, L1_ffn_Wd_s, L1_ffn_Wg, L1_ffn_Wu, L1_ffn_Wd, L1_ffn_Wr, L1_ffn_rb)
    return x

_drawn_inputs = setup_inputs


def setup_inputs(seed=0):
    import zlib

    import numpy as np

    out = dict(_drawn_inputs(seed))
    spreads = {'L0_attn_ln_g': (1.0, 0.2),
     'L0_attn_ln_b': (0.0, 0.1),
     'L1_attn_out_b': (0.0, 0.1),
     'L1_ffn_rb': (0.0, 0.8)}
    factors = {'L0_attn_A_log': 4.011,
     'L0_attn_conv_b': 3.678,
     'L0_ffn_Wg': 8.0,
     'L0_ffn_W1': 8.0,
     'L0_ffn_W2': 8.0,
     'L0_ffn_W3': 8.0,
     'L1_ffn_Wg_s': 7.328,
     'L1_ffn_Wu_s': 7.153,
     'L1_ffn_Wd_s': 7.086,
     'L1_ffn_Wg': 8.0,
     'L1_ffn_Wu': 8.0,
     'L1_ffn_Wd': 8.0,
     'L1_ffn_Wr': 8.0}
    for name, (base, spread) in spreads.items():
        noise = np.random.default_rng([zlib.crc32(name.encode()), seed]).standard_normal(out[name].shape)
        drawn = base * np.exp(spread * noise) if base else spread * noise
        out[name] = jnp.asarray(drawn.astype(out[name].dtype))
    for name, factor in factors.items():
        out[name] = (out[name] * factor).astype(out[name].dtype)
    return out
```

```python
from contextlib import ExitStack

import concourse.bass as bass
from concourse import mybir

ACT = mybir.ActivationFunctionType
ALU = mybir.AluOpType
F32 = mybir.dt.float32
F16 = mybir.dt.float16
BF16 = mybir.dt.bfloat16
U32 = mybir.dt.uint32
AX = mybir.AxisListType.X

P = 128
SEQ = 256
NSEQ = 16
TOK = NSEQ * SEQ
TILES = TOK // P
GROUP = 512
GT = GROUP // P
NG = TOK // GROUP
EPS = 1e-5
WSCALE = 16.0

E0, I0 = 16, 88
E1, I1 = 8, 256
NT0 = E0 * I0 // P
NT1 = (E1 + 1) * I1 // P
LAG = 3
HRING = 6
FRING = 3

HEADS, HD, STATE, TAPS = 4, 64, 64, 4
INNER = HEADS * HD
CH = INNER + 2 * STATE
CS = 256.0
PAD = 4

MAMBA = dict(seg_ready=4, cum_ready=1, g_ready=2, dt_ready=1, yd_ready=2, yoff_ready=1, convx_ready=2, convb_ready=1,
             convc_ready=1, u2_ready=2, hnT_ready=2, y_ready=1,
             decay_ready=4, ed_ready=1, goff_ready=2, e_ready=1, sp_ready=1, bc_biased=2, gelu_ready=2, hnT0_copied=1,
             gm_ready=2, mt_ready=4, dtc_ready=1, d_ready=1, mixed=1, hvar_ready=1, hn_ready=1, xc_biased=2,
             xneg_ready=1, bcneg_ready=2, xs_val=1, bc_val=2, hnT1_copied=1,
             trid_ready=4, xs_ready=1, hrstd_ready=1, x_biased=1)

AH, AD = 16, 8
UNITS = [(0, 0), (1, 0), (1, 1)]
NU = 2 * len(UNITS)
SPREAD = 16 * 24
MAXIMA = 16 * 2
PRING = 3
ROWS = 30
ATTN = dict(s1_ready=NU, max_ready=NU, s2_ready=NU, exp_ready=NU, pv_done=NU, qk_ready=2, rope_mul=2, roped=2,
            part_hi=2, part_lo=2, v_ready=1, v_copied=1, negmax=1, mT_ready=1, mrow_ready=1, onorm=1, oTa_ready=1,
            oTa_copied=1, ya_ready=1)

PER_TILE = ("a_ready", "u_ready", "gx_ready", "silu_ready", "m_ready", "h_ready", "hhi_ready", "hlo_ready", "h_used")
PER_GROUP = ("var_ready", "rstd_ready", "xn_ready", "xnT_ready", "xhi_ready", "xlo_ready", "logits_ready",
             "power_in", "power_out", "gates_ready", "gatesT_ready", "gT_ready", "o_copied",
             "outT_ready", "x_updated")


def build(nc, io, phases):
    ctx = ExitStack()
    with ctx:
        def sb(name, shape, dt=F32):
            return ctx.enter_context(nc.sbuf_tensor(name, shape, dt))

        def bank(name):
            return ctx.enter_context(nc.psum_tensor(name, [P, 512], F32))

        def sem(name):
            return ctx.enter_context(nc.semaphore(name))

        S = {n: sem(n) for n in PER_TILE + PER_GROUP + tuple(MAMBA) + tuple(ATTN)}
        x_loaded = [sem(f"x_loaded{g}") for g in range(NG)]
        consts_loaded, idents_loaded = sem("consts_loaded"), sem("idents_loaded")
        w_loaded = {n: sem(f"{n}_loaded") for n in ("w1g0", "w1u0", "w20", "w1g1", "w1u1", "w21")}
        mamba_loaded, wc_ready, wchi_ready = sem("mamba_loaded"), sem("wc_ready"), sem("wchi_ready")
        attn_loaded, maxima_done = sem("attn_loaded"), sem("maxima_done")
        spread_done = [sem(f"spread_done{k}") for k in range(2)]
        regrouped = sem("regrouped")
        regroup = nc.dram_tensor("regroup", (2, 2, 2, P, SEQ), F16).ap()
        aprep_act, aprep_dve = sem("aprep_act"), sem("aprep_dve")
        mprep_act, mprep_dve = sem("mprep_act"), sem("mprep_dve")
        whi_ready, wlo_ready, out_stored = sem("whi_ready"), sem("wlo_ready"), sem("out_stored")
        dve_step, pool_step = sem("dve_step"), sem("pool_step")

        class Arena:
            def __init__(self, name, words):
                self.mem, self.words, self.at = sb(name, [P, words]), words, 0

            def restart(self):
                self.at = 0

            def take(self, shape, dt=F32):
                n = 1
                for d in shape[1:]:
                    n *= d
                words = n * (1 if dt == F32 else 2) // (1 if dt == F32 else 4)
                v = self.mem[0:shape[0], self.at:self.at + words]
                self.at += words
                assert self.at <= self.words
                if dt != F32:
                    v = v.bitcast(dt)
                names = "abcd"[:len(shape) - 1]
                return v.rearrange(f"p ({' '.join(names)}) -> p {' '.join(names)}", **dict(zip(names, shape[1:])))

        tiles_mem, tokens_mem = Arena("tiles_mem", 7168), Arena("tokens_mem", TOK)
        stage_mem, conv_mem = Arena("stage_mem", NT1 * P), Arena("conv_mem", CH // P * TAPS * CH)
        x = sb("x", [P, TILES, P])
        xn = sb("xn", [P, GT, P])
        xhi, xlo = tokens_mem.take([P, TOK], F16), tokens_mem.take([P, TOK], F16)
        stats, mv = sb("stats", [P, GT, 6]), sb("mv", [P, GT, 2])
        vpe, rstd = sb("vpe", [P, GT]), sb("rstd", [P, GT])
        neghalf, eps, euler = sb("neghalf", [P, GT]), sb("eps", [P, GT]), sb("euler", [P, GT, E1])
        ident, identb = sb("ident", [P, P]), sb("identb", [P, P], BF16)
        experts = sb("experts", [P, GT, E0])
        stage = stage_mem.take([P, NT1 * P])
        W = {}
        for k, nt in ((0, NT0), (1, NT1)):
            for n in ("w1g", "w1u", "w2"):
                W[n, k] = (sb(f"{n}{k}hi", [P, nt * P], F16), sb(f"{n}{k}lo", [P, nt * P], F16))
        sel = {0: sb("sel0", [P, NT0 * P], BF16), 1: sb("sel1", [P, NT1 * P], BF16)}
        wr = {0: sb("wr0", [P, E0]), 1: sb("wr1", [P, E1])}
        wrs = {0: sb("wrs0", [P, 2, E0], F16), 1: sb("wrs1", [P, 2, E1], F16)}
        rb = sb("rb", [P, E1])
        lg = sb("lg", [P, GT, E0])
        top = sb("top", [P, GT, 8])
        topi = sb("topi", [P, GT, 8], U32)
        topf = sb("topf", [P, GT, 2])
        pin, pout = sb("pin", [P, GT, E1]), sb("pout", [P, GT, E1])
        gw = sb("gw", [P, GT, 2])
        eq = sb("eq", [P, 2, GT, E0])
        gate = sb("gate", [P, GT, E0])
        gres = sb("gres", [P, GT, E0])
        gparts = sb("gparts", [P, GT, P], BF16)
        gT = sb("gT", [P, TOK], BF16)
        silu = tiles_mem.take([P, 2, 512])
        m = tiles_mem.take([P, 2, 512])
        h = tiles_mem.take([P, FRING, 512])
        hhi, hlo = tiles_mem.take([P, HRING, 512], F16), tiles_mem.take([P, HRING, 512], F16)
        oT = tiles_mem.take([P, 512])

        tri, later = sb("tri", [P, P]), sb("later", [P, P])
        win1 = sb("win1", [P, CH // P, P])
        convw = conv_mem.take([P, CH // P, TAPS, CH])
        wc = [sb("wchi", [P, TAPS, CH], F16), sb("wclo", [P, TAPS, CH], F16)]
        wdt, win2, w3 = sb("wdt", [P, HEADS]), sb("win2", [P, INNER]), sb("w3", [P, 2, P])
        wdts, win2s = sb("wdts", [P, 2, HEADS], F16), sb("win2s", [P, 2, INNER], F16)
        lng, lnb = sb("lng", [P, 2]), sb("lnb", [P, 2])
        lnbw, w3g, b3 = sb("lnbw", [P, 2, P]), sb("w3g", [P, 2, P]), sb("b3", [P, P])
        xbias, bcbias, slope = sb("xbias", [P, INNER]), sb("bcbias", [STATE, 2]), sb("slope", [P, 1])
        alog, rate = sb("alog", [P, HEADS]), sb("rate", [P, HEADS])
        xm = [sb("xmhi", [P, 2, PAD + SEQ], F16), sb("xmlo", [P, 2, PAD + SEQ], F16)]
        dt, dtc, dtx, de, sp, dd = (sb(n, [P, GT, HEADS]) for n in ("dt", "dtc", "dtx", "de", "sp", "dd"))
        for arena in (tiles_mem, tokens_mem, stage_mem, conv_mem):
            arena.restart()
        trid, decay, mt = (tiles_mem.take([P, GT, HEADS * P]) for _ in range(3))
        ed = sb("ed", [P, 2, 2, HEADS])
        gm, goff = sb("gm", [P, GT, P]), sb("goff", [P, 2, P])
        xc, xneg, xv, hm = (tokens_mem.take([P, GT, INNER]) for _ in range(4))
        bcc, bcneg, bcv = (conv_mem.take([STATE, 2, GROUP]) for _ in range(3))
        xsd = conv_mem.take([P, 2, INNER])
        u2 = tiles_mem.take([P, GT, INNER])
        yo = conv_mem.take([P, 2, INNER])
        hn = stage_mem.take([P, GT, INNER])
        hnT = stage_mem.take([P, 2, GROUP])
        hstats, hmv, hvpe, hrstd = sb("hstats", [P, GT, 6]), sb("hmv", [P, GT, 2]), sb("hvpe", [P, GT]), sb("hrstd", [P, GT])

        qa, ka = ([sb(f"{n}{k}", [P, 4, SEQ], F16) for k in range(2)] for n in ("qa", "ka"))
        xa = [sb("xahi", [P, GROUP], F16), sb("xalo", [P, GROUP], F16)]
        ropec, ropes = sb("ropec", [P, SEQ]), sb("ropes", [P, SEQ])
        maskq, maskk = sb("maskq", [P, 512], BF16), sb("maskk", [P, 512], BF16)
        identh = sb("identh", [P, P], F16)
        wqk, wv = sb("wqk", [P, 4 * P]), sb("wv", [P, P])
        wqks, wvs = sb("wqks", [P, 2, 4 * P], F16), sb("wvs", [P, 2, P], F16)
        wo, obias = sb("wo", [P, P]), sb("obias", [P, P])
        tiles_mem.restart(), tokens_mem.restart()
        pt = tiles_mem.take([P, PRING, 1024])
        rope = tiles_mem.take([P, 2, 2, SEQ])
        qk = tiles_mem.take([P, 2, SEQ])
        qks = tiles_mem.take([P, 2, 2, SEQ], F16)
        va = tokens_mem.take([P, 2, 2, AH * (AD + 1)])
        mx = tokens_mem.take([P, 3, AH])
        negm = tokens_mem.take([P, 2, AH])
        mparts = tokens_mem.take([P, 2, 2 * AH], F16)
        mrow = tokens_mem.take([2 * 4, 4, SEQ], F16)
        orec = tokens_mem.take([P, 2, AH])
        on = tokens_mem.take([P, 2, P])
        oTa = tokens_mem.take([P, SEQ])

        sets = [ctx.enter_context(nc.psum_tensor(f"set{k}", [P, 1024], F32)) for k in range(3)]
        bA, bU, bG = ([s[:, 0:512], s[:, 512:1024]] for s in sets)
        bO, bT = bank("bO"), bank("bT")
        bTh = bT[:, :].bitcast(F16)
        mX, mB, mC, mU, mY = [bA[0], bO], bU[0], bU[1], bG, bA[1]
        mSeg, mG, mCum = [bG[0], bG[1], bU[0], bU[1]], [bO, bA[0]], bA[1]
        bTb = bT[:, :].bitcast(BF16)

        NT = {"F0": NT0, "F1": NT1}
        SHARED = ("var_ready", "rstd_ready", "xn_ready", "xnT_ready", "xhi_ready", "xlo_ready", "x_updated")
        base = []
        tally = {n: 0 for n in S}
        for ph in phases:
            base.append(dict(tally))
            if ph in NT:
                for n in PER_TILE:
                    tally[n] += NG * NT[ph]
                for n in PER_GROUP:
                    tally[n] += NG
            else:
                for n in SHARED:
                    tally[n] += NG
                if ph == "M":
                    for n, k in MAMBA.items():
                        tally[n] += NG * k
                else:
                    for n, k in ATTN.items():
                        tally[n] += NSEQ * k
                    tally["x_updated"] += NSEQ - NG
                    tally["x_biased"] += NG

        def wait(eng, name, value):
            if not isinstance(value, int) or value > 0:
                eng.wait_ge(S[name], value)

        def wait_apart(eng, name, value):
            if not isinstance(value, int):
                eng.wait_ge(consts_loaded, ALL_CONSTS)
            wait(eng, name, value)

        class Chain:
            def __init__(self, eng, s):
                self.eng, self.s, self.at, self.k = eng, s, 0, 0

            def add(self, ins):
                ins.then_inc(self.s, 1)
                self.k += 1

            def join(self):
                self.eng.drain()

            def link(self, ins):
                self.add(ins)
                self.join()

        def groups(eng, emit, chain=None, per=0):
            emit(0)
            if chain:
                start = chain.at + chain.k
                chain.k = 0
            with eng.Fori(1, NG - 1) as g:
                if chain:
                    chain.at = start + (g - 1) * per
                emit(g)
                if chain:
                    assert chain.k == per, chain.k
            if chain:
                chain.at, chain.k = start + (NG - 2) * per, 0
            emit(NG - 1)

        class Seq:
            def __init__(self, value, index=None, half=None):
                self.value = value
                self.half = value // 2 if half is None else half
                self.index = value if index is None else index
                self.parity = self.index % 2

            def plus(self, n):
                return Seq(self.value + n, self.index + n, self.half + (self.parity + n) // 2)

        def steps(eng, step):
            with eng.Fori(0, NG - 1) as g:
                for s in range(2):
                    step(Seq(2 * g + s, 2 + s, g))
            for q in (NSEQ - 2, NSEQ - 1):
                step(Seq(q))

        def is_first(g):
            return isinstance(g, int) and g == 0

        def is_last(g):
            return isinstance(g, int) and g == NG - 1

        MLOADS = [("tri", tri), ("later", later), ("win1", win1), ("convw", convw), ("wdt", wdt), ("win2", win2), ("w3", w3),
                  ("lng", lng), ("lnb", lnb), ("xbias", xbias), ("bcbias", bcbias), ("slope", slope), ("alog", alog)]
        ALOADS = [("qinit", qa[0]), ("qinit", qa[1]), ("kinit", ka[0]), ("kinit", ka[1]), ("ropec", ropec), ("ropes", ropes),
                  ("maskq", maskq), ("maskk", maskk), ("identh", identh), ("wqk", wqk), ("wv", wv), ("wo", wo), ("obias", obias)]
        ALL_ALOADS = 16 * len(ALOADS)
        ALL_MLOADS = 16 * len(MLOADS)

        def pair(buf):
            return buf[:, :, PAD:]

        block = ctx.enter_context(nc.Block())
        x_dram = io["x"].rearrange("b (h p) d -> p (b h) d", p=P)
        y_dram = io["out"].rearrange("b (h p) d -> p (b h) d", p=P)

        WEIGHTS = [(n, k) for k in (0, 1) for n in ("w1g", "w1u", "w2")]
        CONSTS = [("experts", experts[:, :, :]), ("sel0", sel[0][:, :]), ("sel1", sel[1][:, :]),
                  ("wr0", wr[0][:, :]), ("wr1", wr[1][:, :]), ("rb", rb[:, :])]
        ALL_CONSTS = 16 * len(CONSTS)

        @block.sync
        def _(sp):
            for n, dst in (("ident", ident), ("identb", identb)):
                sp.dma_start(dst[:, :], io[n]).then_inc(idents_loaded, 16)
            for g in range(NG):
                sp.dma_start(x[:, g * GT:(g + 1) * GT, :], x_dram[:, g * GT:(g + 1) * GT, :]).then_inc(x_loaded[g], 16)
            for n, dst in MLOADS:
                src = io[n].partition_broadcast(P) if n in ("xbias", "slope", "alog") else io[n]
                sp.dma_start(dst[tuple([slice(None)] * len(dst.shape))], src).then_inc(mamba_loaded, 16)
            for n, dst in ALOADS:
                src = io[n].partition_broadcast(P) if n == "obias" else io[n]
                sp.dma_start(dst[tuple([slice(None)] * len(dst.shape))], src).then_inc(attn_loaded, 16)

            def attention(b):
                def spread(q):
                    for n in range(2):
                        if n == 0 and q.index >= 2:
                            wait_apart(sp, "s2_ready", b["s2_ready"] + NU * (q.value - 1))
                        wait_apart(sp, "part_lo", b["part_lo"] + 2 * q.value + n + 1)
                        sp.dma_start(regroup[q.parity, n].rearrange("a p s -> p a s"), qks[:, n, :, :]).then_inc(regrouped, 16)
                    for n, buf in ((0, qa), (1, ka)):
                        sp.wait_ge(consts_loaded, ALL_CONSTS)
                        sp.wait_ge(regrouped, 32 * (q.value + 1))
                        for c in range(3):
                            src = regroup[q.parity, n, int(c == (1, 2)[n])].rearrange("(i j e) s -> i e j s", i=4, j=4)
                            for i in range(4):
                                r = 32 * i + AD * c
                                sp.dma_start(buf[q.parity][r:r + AD, :, :], src[i]).then_inc(spread_done[q.parity], 16)

                def maxima(q):
                    wait_apart(sp, "mrow_ready", b["mrow_ready"] + q.value + 1)
                    for c in range(2):
                        sp.dma_start(qa[q.parity][ROWS + c::32, :, :], mrow[4 * c:4 * c + 4, :, :]).then_inc(maxima_done, 16)

                def step(q):
                    if q.index < NSEQ - 2:
                        spread(q.plus(2))
                    if q.index < NSEQ - 1:
                        maxima(q.plus(1))
                spread(Seq(0))
                spread(Seq(1))
                maxima(Seq(0))
                steps(nc.sync, step)
            for ph, b in zip(phases, base):
                if ph == "A":
                    attention(b)
            sp.wait_ge(S["x_updated"], tally["x_updated"])
            sp.dma_start(y_dram, x[:, :, :]).then_inc(out_stored, 16)
            sp.wait_ge(out_stored, 16)

        @block.gpsimd
        def _(pool):
            ch = Chain(pool, pool_step)
            ch.add(pool.memset(gT[:, :].bitcast(U32), 0))
            ch.add(pool.memset(gparts[:, :, :].bitcast(U32), 0))
            ch.add(pool.memset(eps[:, :], EPS))
            ch.add(pool.memset(neghalf[:, :], -0.5))
            ch.add(pool.memset(euler[:, :, :], 2.718281828459045))
            for n, dst in CONSTS:
                src = io[n].partition_broadcast(P) if n == "rb" else io[n]
                pool.dma_start(dst, src).then_inc(consts_loaded, 16)
            for n, (name, k) in enumerate(WEIGHTS):
                nt = (NT0, NT1)[k]
                if n:
                    pool.wait_ge(wlo_ready, n)
                pool.dma_start(stage[:, 0:nt * P], io[f"{name}{k}"]).then_inc(w_loaded[f"{name}{k}"], 16)
            ch.join()

            def rsqrt(b, g):
                wait(pool, "var_ready", b["var_ready"] + g + 1)
                ch.link(pool.tensor_tensor(vpe[:, :], mv[:, :, 1], eps[:, :], ALU.add))
                pool.tensor_tensor(rstd[:, :], vpe[:, :], neghalf[:, :], ALU.pow).then_inc(S["rstd_ready"], 1)

            def powers(b, g, kind):
                wait(pool, "power_in", b["power_in"] + g + 1)
                n = 1 if kind == "F0" else E1
                pool.tensor_tensor(pout[:, :, 0:n], euler[:, :, 0:n], pin[:, :, 0:n], ALU.pow).then_inc(S["power_out"], 1)

            def layer(kind, b):
                nt = NT[kind]

                def group(g):
                    for j in range(nt):
                        t = nt * g + j
                        wait(pool, "hhi_ready", b["hhi_ready"] + t + 1)
                        r, f = j % HRING, j % FRING
                        pool.tensor_tensor(hlo[:, r, :], h[:, f, :], hhi[:, r, :], ALU.subtract).then_inc(S["hlo_ready"], 1)
                        if not is_last(g):
                            if j == 0:
                                rsqrt(b, g + 1)
                            if j == 7:
                                powers(b, g + 1, kind)
                rsqrt(b, 0)
                powers(b, 0, kind)
                groups(nc.gpsimd, group, ch, 1)

            def mamba(b):
                def x_bias(g):
                    wait(pool, "xn_ready", b["xn_ready"] + g + 1)
                    dst = x[:, bass.ts(g, GT), :]
                    pool.tensor_tensor(dst, dst, b3[:, :].unsqueeze(1).broadcast_to([P, GT, P]), ALU.add).then_inc(S["x_biased"], 1)

                def hidden_rsqrt(g):
                    wait(pool, "hvar_ready", b["hvar_ready"] + g + 1)
                    ch.link(pool.tensor_tensor(hvpe[:, :], hmv[:, :, 1], eps[:, :], ALU.add))
                    pool.tensor_tensor(hrstd[:, :], hvpe[:, :], neghalf[:, :], ALU.pow).then_inc(S["hrstd_ready"], 1)

                def scaled_x(g):
                    wait(pool, "ed_ready", b["ed_ready"] + g + 1)
                    wait(pool, "xs_val", b["xs_val"] + g + 1)
                    wait(pool, "yoff_ready", b["yoff_ready"] + g)
                    for q in range(2):
                        ins = pool.tensor_tensor(xsd[:, q, :].rearrange("p (h d) -> p h d", d=HD),
                                                 xv[:, 2 * q, :].rearrange("p (h d) -> p h d", d=HD),
                                                 ed[:, 0, q, :].unsqueeze(2).broadcast_to([P, HEADS, HD]), ALU.mult)
                    ins.then_inc(S["xs_ready"], 1)

                def triangles(g):
                    wait(pool, "d_ready", b["d_ready"] + g + 1)
                    for t in range(GT):
                        wait(pool, "seg_ready", b["seg_ready"] + GT * g - GT + t + 1 if not is_first(g) else b["seg_ready"])
                        pool.tensor_tensor(trid[:, t, :].rearrange("p (h l) -> p h l", l=P),
                                           tri[:, :].unsqueeze(1).broadcast_to([P, HEADS, P]),
                                           dd[:, t, :].unsqueeze(2).broadcast_to([P, HEADS, P]), ALU.mult).then_inc(S["trid_ready"], 1)

                def body(g):
                    nxt = not is_last(g)
                    if nxt:
                        rsqrt(b, g + 1)
                    scaled_x(g)
                    if nxt:
                        x_bias(g + 1)
                    hidden_rsqrt(g)
                    if nxt:
                        triangles(g + 1)
                pool.wait_ge(mamba_loaded, ALL_MLOADS)
                pool.wait_ge(mprep_act, 3)
                rsqrt(b, 0)
                x_bias(0)
                triangles(0)
                with nc.gpsimd.Fori(0, NG - 1) as g:
                    body(g)
                body(NG - 1)

            def attention(b):
                def x_bias(g):
                    wait(pool, "xn_ready", b["xn_ready"] + g + 1)
                    dst = x[:, bass.ts(g, GT), :]
                    pool.tensor_tensor(dst, dst, obias[:, :].unsqueeze(1).broadcast_to([P, GT, P]), ALU.add).then_inc(S["x_biased"], 1)

                def rope_sum(q):
                    for n in range(2):
                        t = 2 * q.value + n
                        wait(pool, "rope_mul", b["rope_mul"] + t + 1)
                        pool.tensor_tensor(qk[:, n, :], rope[:, n, 0, :], rope[:, n, 1, :], ALU.add).then_inc(S["roped"], 1)
                        wait(pool, "part_hi", b["part_hi"] + t + 1)
                        pool.tensor_tensor(qks[:, n, 1, :], qk[:, n, :], qks[:, n, 0, :], ALU.subtract).then_inc(S["part_lo"], 1)

                def step(q):
                    if q.index < NSEQ - 2:
                        if q.parity == 0:
                            rsqrt(b, q.half + 1)
                            x_bias(q.half + 1)
                        rope_sum(q.plus(2))
                pool.wait_ge(attn_loaded, ALL_ALOADS)
                rsqrt(b, 0)
                x_bias(0)
                rope_sum(Seq(0))
                rope_sum(Seq(1))
                steps(nc.gpsimd, step)
            for ph, b in zip(phases, base):
                {"M": mamba, "A": attention}[ph](b) if ph in "MA" else layer(ph, b)

        def last_user(nt, j, n):
            if j >= n:
                return j - n
            return max(i for i in range(nt) if i % n == j % n) - nt

        def wait_slot(eng, name, b, nt, g, j, n):
            prev = last_user(nt, j, n)
            if is_first(g) and prev < 0:
                wait(eng, name, b[name])
            else:
                wait(eng, name, b[name] + nt * g + prev + 1)

        @block.scalar
        def _(act):
            for n, (name, k) in enumerate(WEIGHTS):
                nt = (NT0, NT1)[k]
                act.wait_ge(w_loaded[f"{name}{k}"], 16)
                act.activation(W[name, k][0][:, :], stage[:, 0:nt * P], ACT.Copy, scale=WSCALE).then_inc(whi_ready, 1)
            act.wait_ge(consts_loaded, ALL_CONSTS)
            for k in (0, 1):
                act.activation(wrs[k][:, 0, :], wr[k][:, :], ACT.Copy, scale=WSCALE).then_inc(whi_ready, 1)

            def x_hi(b, g):
                wait(act, "xnT_ready", b["xnT_ready"] + g + 1)
                act.activation(xhi[:, bass.ts(g, GROUP)], bT[:, :], ACT.Copy).then_inc(S["xhi_ready"], 1)

            def gates_out(b, g, kg):
                wait(act, "gatesT_ready", b["gatesT_ready"] + g + 1)
                act.activation(gT[0:kg, bass.ts(g, GROUP)], bTb[0:kg, 0:GROUP], ACT.Copy).then_inc(S["gT_ready"], 1)

            def out_copy(b, g, nt):
                wait(act, "h_used", b["h_used"] + nt * (g + 1))
                wait(act, "outT_ready", b["outT_ready"] + g)
                act.activation(oT[:, :], bO[:, :], ACT.Copy, scale=0.5 / WSCALE ** 2).then_inc(S["o_copied"], 1)

            def layer(kind, b):
                nt, kg = NT[kind], 3 * (E0 if kind == "F0" else E1 + 1)

                def h_hi(g, j, t):
                    wait(act, "h_ready", b["h_ready"] + t + 1)
                    wait_slot(act, "h_used", b, nt, g if j >= 0 else g - 1, j % nt, HRING)
                    act.activation(hhi[:, j % nt % HRING, :], h[:, j % nt % FRING, :], ACT.Copy).then_inc(S["hhi_ready"], 1)

                def group(g):
                    for j in range(nt):
                        t = nt * g + j
                        wait(act, "a_ready", b["a_ready"] + t + 1)
                        wait_slot(act, "m_ready", b, nt, g, j, 2)
                        act.activation(silu[:, j % 2, :], bA[j % 2][:, :], ACT.Silu, scale=1.0 / WSCALE).then_inc(S["silu_ready"], 1)
                        if j > 0:
                            h_hi(g, j - 1, t - 1)
                        if j == 2 and not is_first(g):
                            out_copy(b, g - 1, nt)
                        if not is_last(g):
                            if j == 5:
                                x_hi(b, g + 1)
                            if j == 10:
                                gates_out(b, g + 1, kg)
                    h_hi(g, nt - 1, nt * g + nt - 1)
                x_hi(b, 0)
                gates_out(b, 0, kg)
                groups(nc.scalar, group)
                out_copy(b, NG - 1, nt)

            def mamba(b):
                def prepare():
                    act.wait_ge(mamba_loaded, ALL_MLOADS)
                    act.activation(rate[:, :], alog[:, :], ACT.Exp).then_inc(mprep_act, 1)
                    act.wait_ge(wc_ready, TAPS + 1)
                    act.activation(b3[:, :], bT[:, 0:P], ACT.Copy).then_inc(mprep_act, 1)
                    for k in range(TAPS):
                        act.activation(wc[0][:, k, :], [bA[0], bA[1], bU[0], bU[1]][k][:, 0:CH], ACT.Copy, scale=CS).then_inc(wchi_ready, 1)
                    act.activation(wdts[:, 0, :], wdt[:, :], ACT.Copy, scale=CS).then_inc(wchi_ready, 1)
                    act.activation(win2s[:, 0, :], win2[:, :], ACT.Copy, scale=CS).then_inc(mprep_act, 1)

                def decays(g):
                    for t in range(GT):
                        wait(act, "seg_ready", b["seg_ready"] + GT * g + t + 1)
                        wait(act, "mt_ready", b["mt_ready"] + GT * g)
                        act.activation(decay[:, t, :], mSeg[t][:, :], ACT.Exp, scale=-1.0).then_inc(S["decay_ready"], 1)
                    wait(act, "cum_ready", b["cum_ready"] + g + 1)
                    wait(act, "mixed", b["mixed"] + g)
                    act.activation(ed[:, :, :, :], mCum[:, 0:4 * HEADS].rearrange("p (a q h) -> p a q h", a=2, q=2),
                                   ACT.Exp, scale=-1.0).then_inc(S["ed_ready"], 1)

                def g_off(g):
                    for q in range(2):
                        wait(act, "gm_ready", b["gm_ready"] + 2 * g + q + 1)
                        wait(act, "yoff_ready", b["yoff_ready"] + g)
                        act.activation(goff[:, q, :], mG[q][:, P:2 * P], ACT.Copy).then_inc(S["goff_ready"], 1)

                def x_hi_pair(g):
                    wait(act, "xnT_ready", b["xnT_ready"] + g + 1)
                    wait(act, "u2_ready", b["u2_ready"] + 2 * g)
                    act.activation(pair(xm[0]), bT[:, :].rearrange("p (q s) -> p q s", q=2), ACT.Copy).then_inc(S["xhi_ready"], 1)

                def softplus(g):
                    wait(act, "dtc_ready", b["dtc_ready"] + g + 1)
                    act.activation(de[:, :, :], dtc[:, :, :], ACT.Exp).then_inc(S["e_ready"], 1)
                    wait(act, "e_ready", b["e_ready"] + g + 1)
                    act.activation(sp[:, :, :], de[:, :, :], ACT.Ln, bias=1.0).then_inc(S["sp_ready"], 1)

                def bc_bias(g):
                    for n, (s, bk) in enumerate((("convb_ready", mB), ("convc_ready", mC))):
                        wait(act, s, b[s] + g + 1)
                        wait(act, "bc_val", b["bc_val"] + 2 * g)
                        act.activation(bcc[:, n, :], bk[0:STATE, :], ACT.Identity, scale=1.0 / CS, bias=bcbias[:, n:n + 1]).then_inc(S["bc_biased"], 1)

                def gelu(g):
                    for n in range(2):
                        wait(act, "u2_ready", b["u2_ready"] + 2 * g + n + 1)
                        wait(act, "mixed", b["mixed"] + g)
                        act.activation(u2[:, 2 * n:2 * n + 2, :], mU[n][:, :].rearrange("p (t c) -> p t c", t=2), ACT.Gelu, scale=1.0 / CS)\
                           .then_inc(S["gelu_ready"], 1)

                def hnT_copy(g):
                    wait(act, "hnT_ready", b["hnT_ready"] + 2 * g + 1)
                    wait(act, "y_ready", b["y_ready"] + g)
                    act.activation(hnT[:, 0, :], mY[:, :], ACT.Copy).then_inc(S["hnT0_copied"], 1)

                def body(g):
                    nxt = not is_last(g)
                    decays(g)
                    g_off(g)
                    if nxt:
                        x_hi_pair(g + 1)
                        softplus(g + 1)
                        bc_bias(g + 1)
                        gelu(g + 1)
                    hnT_copy(g)
                prepare()
                x_hi_pair(0)
                softplus(0)
                bc_bias(0)
                gelu(0)
                with nc.scalar.Fori(0, NG - 1) as g:
                    body(g)
                body(NG - 1)

            def attention(b):
                def prepare():
                    act.wait_ge(attn_loaded, ALL_ALOADS)
                    act.activation(wqks[:, 0, :], wqk[:, :], ACT.Copy, scale=WSCALE).then_inc(aprep_act, 1)
                    act.activation(wvs[:, 0, :], wv[:, :], ACT.Copy, scale=WSCALE).then_inc(aprep_act, 1)

                def x_hi_pair(g):
                    wait(act, "xnT_ready", b["xnT_ready"] + g + 1)
                    wait(act, "v_ready", b["v_ready"] + 2 * g)
                    act.activation(xa[0][:, :], bT[:, :], ACT.Copy).then_inc(S["xhi_ready"], 1)

                def part_hi(q):
                    for n in range(2):
                        t = 2 * q.value + n
                        wait(act, "roped", b["roped"] + t + 1)
                        if q.index >= 1:
                            act.wait_ge(regrouped, 32 * q.value)
                        act.activation(qks[:, n, 0, :], qk[:, n, :], ACT.Copy).then_inc(S["part_hi"], 1)

                def v_copy(q):
                    wait(act, "v_ready", b["v_ready"] + q.value + 1)
                    if q.index >= 2:
                        wait(act, "pv_done", b["pv_done"] + NU * (q.value - 1))
                    for t in range(2):
                        dst = va[:, q.parity, t, :].rearrange("p (h e) -> p h e", e=AD + 1)[:, :, 0:AD]
                        ins = act.activation(dst, bT[:, t * P:(t + 1) * P].rearrange("p (h e) -> p h e", e=AD), ACT.Copy, scale=1.0 / WSCALE)
                    ins.then_inc(S["v_copied"], 1)

                def exps(q, u):
                    wait(act, "s2_ready", b["s2_ready"] + NU * q.value + u + 1)
                    act.activation(pt[:, u % PRING, :], sets[2 * u % 3][:, :], ACT.Exp, scale=AD ** -0.5).then_inc(S["exp_ready"], 1)

                def m_copy(q):
                    wait(act, "mT_ready", b["mT_ready"] + q.value + 1)
                    if q.index >= 1:
                        act.wait_ge(maxima_done, MAXIMA * q.value)
                    act.activation(mrow[:, :, :], bTh[0:8, :].rearrange("p (j s) -> p j s", j=4), ACT.Copy).then_inc(S["mrow_ready"], 1)

                def o_copy(q):
                    wait(act, "oTa_ready", b["oTa_ready"] + q.value + 1)
                    wait(act, "ya_ready", b["ya_ready"] + q.value)
                    act.activation(oTa[:, :], bT[:, 0:SEQ], ACT.Copy).then_inc(S["oTa_copied"], 1)

                def step(q):
                    front, back = q.index < NSEQ - 2, q.index < NSEQ - 1
                    for u in range(NU):
                        exps(q, u)
                        if front:
                            if u == 0 and q.parity == 0:
                                x_hi_pair(q.half + 1)
                            if u == 4:
                                part_hi(q.plus(2))
                    if front:
                        v_copy(q.plus(2))
                    if back:
                        m_copy(q.plus(1))
                    o_copy(q)
                prepare()
                x_hi_pair(0)
                for q in (Seq(0), Seq(1)):
                    part_hi(q)
                    v_copy(q)
                m_copy(Seq(0))
                steps(nc.scalar, step)
            for ph, b in zip(phases, base):
                {"M": mamba, "A": attention}[ph](b) if ph in "MA" else layer(ph, b)

        @block.vector
        def _(dve):
            ch = Chain(dve, dve_step)
            for n, (name, k) in enumerate(WEIGHTS):
                nt = (NT0, NT1)[k]
                dve.wait_ge(whi_ready, n + 1)
                dve.scalar_tensor_tensor(W[name, k][1][:, :], stage[:, 0:nt * P], WSCALE, W[name, k][0][:, :],
                                         ALU.mult, ALU.subtract).then_inc(wlo_ready, 1)
            dve.wait_ge(whi_ready, len(WEIGHTS) + 2)
            for k in (0, 1):
                dve.scalar_tensor_tensor(wrs[k][:, 1, :], wr[k][:, :], WSCALE, wrs[k][:, 0, :],
                                         ALU.mult, ALU.subtract).then_inc(wlo_ready, 1)

            def xs(g, i):
                return x[:, bass.ds(GT * g + i, 1), :].squeeze(1) if not isinstance(g, int) else x[:, GT * g + i, :]

            def ln_stats(b, g):
                for i in range(GT):
                    ch.add(dve.bn_stats(stats[:, i, :], xs(g, i)))
                ch.join()
                for i in range(GT):
                    ins = dve.bn_aggr(mv[:, i, :], stats[:, i, :])
                    if i < GT - 1:
                        ch.add(ins)
                    else:
                        ins.then_inc(S["var_ready"], 1)

            def ln_apply(b, g):
                wait_apart(dve, "var_ready", b["var_ready"] + g + 1)
                wait(dve, "rstd_ready", b["rstd_ready"] + g + 1)
                wait(dve, "xnT_ready", b["xnT_ready"] + g)
                for i in range(GT):
                    ins = dve.tensor_scalar(xn[:, i, :], xs(g, i), mv[:, i, 0:1], rstd[:, i:i + 1], ALU.subtract, ALU.mult)
                    if i < GT - 1:
                        ch.add(ins)
                    else:
                        ins.then_inc(S["xn_ready"], 1)

            def x_lo(b, g):
                wait(dve, "xhi_ready", b["xhi_ready"] + g + 1)
                dve.tensor_tensor(xlo[:, bass.ts(g, GROUP)], bT[:, :], xhi[:, bass.ts(g, GROUP)],
                                  ALU.subtract).then_inc(S["xlo_ready"], 1)

            def find_top(src, n):
                for i in range(GT):
                    ch.add(dve.max(top[:, i, :], src[:, i, 0:n]))
                ch.join()
                for i in range(GT):
                    ch.add(dve.max_index(topi[:, i, :], top[:, i, :], src[:, i, 0:n]))
                ch.join()
                ch.link(dve.tensor_copy(topf[:, :, :], topi[:, :, 0:2]))

            def route_begin(b, g, kind):
                wait(dve, "logits_ready", b["logits_ready"] + g + 1)
                wait(dve, "power_out", b["power_out"] + g)
                if kind == "F0":
                    ps = bT[:, 0:GT * E0].rearrange("p (t e) -> p t e", e=E0)
                    ch.link(dve.tensor_scalar(lg[:, :, :], ps, 1.0 / WSCALE, None, ALU.mult))
                    find_top(lg, E0)
                    dve.tensor_tensor(pin[:, :, 0], top[:, :, 1], top[:, :, 0], ALU.subtract).then_inc(S["power_in"], 1)
                else:
                    ps = bT[:, 0:GT * E1].rearrange("p (t e) -> p t e", e=E1)
                    ch.link(dve.tensor_scalar(lg[:, :, 0:E1], ps, -1.0 / WSCALE, None, ALU.mult))
                    dve.tensor_tensor(pin[:, :, :], lg[:, :, 0:E1], rb[:, :].unsqueeze(1).broadcast_to([P, GT, E1]),
                                      ALU.subtract).then_inc(S["power_in"], 1)

            def route_end(b, g, kind):
                wait(dve, "power_out", b["power_out"] + g + 1)
                wait(dve, "power_in", b["power_in"] + g + 1)
                if kind == "F0":
                    n, ne = E0, E0
                    ch.link(dve.tensor_scalar(gw[:, :, 1], pout[:, :, 0], 1.0, None, ALU.add))
                    ch.link(dve.reciprocal(gw[:, :, 0], gw[:, :, 1]))
                    ch.link(dve.tensor_tensor(gw[:, :, 1], pout[:, :, 0], gw[:, :, 0], ALU.mult))
                    weight = [gw[:, :, k:k + 1] for k in (0, 1)]
                else:
                    n, ne = E1, E1 + 1
                    ch.link(dve.tensor_scalar(lg[:, :, 0:E1], pout[:, :, :], 1.0, None, ALU.add))
                    ch.link(dve.reciprocal(lg[:, :, 0:E1], lg[:, :, 0:E1]))
                    find_top(lg, E1)
                    weight = [top[:, :, k:k + 1] for k in (0, 1)]
                for k in (0, 1):
                    ch.add(dve.tensor_tensor(eq[:, k, :, 0:n], experts[:, :, 0:n], topf[:, :, k:k + 1].broadcast_to([P, GT, n]),
                                             ALU.is_equal))
                ch.join()
                for k in (0, 1):
                    ch.add(dve.tensor_tensor(eq[:, k, :, 0:n], eq[:, k, :, 0:n], weight[k].broadcast_to([P, GT, n]), ALU.mult))
                ch.join()
                ch.link(dve.tensor_tensor(gate[:, :, 0:n], eq[:, 0, :, 0:n], eq[:, 1, :, 0:n], ALU.add))
                wait(dve, "gatesT_ready", b["gatesT_ready"] + g)
                if kind == "F1":
                    ch.link(dve.memset(gate[:, :, E1:E1 + 1], 1.0))
                part = [gparts[:, :, k * ne:(k + 1) * ne] for k in range(3)]
                ch.link(dve.tensor_copy(part[0], gate[:, :, 0:ne]))
                ch.link(dve.tensor_tensor(gres[:, :, 0:ne], gate[:, :, 0:ne], part[0], ALU.subtract))
                ch.link(dve.tensor_copy(part[1], gres[:, :, 0:ne]))
                dve.tensor_tensor(part[2], gres[:, :, 0:ne], part[1], ALU.subtract).then_inc(S["gates_ready"], 1)

            def x_update(b, g):
                wait(dve, "outT_ready", b["outT_ready"] + g + 1)
                dst = x[:, bass.ts(g, GT), :]
                dve.tensor_tensor(dst, dst, bT[:, :].rearrange("p (t d) -> p t d", d=P), ALU.add).then_inc(S["x_updated"], 1)

            def layer(kind, b, per):
                nt = NT[kind]

                def group(g):
                    for j in range(nt):
                        t = nt * g + j
                        wait(dve, "silu_ready", b["silu_ready"] + t + 1)
                        wait(dve, "u_ready", b["u_ready"] + t + 1)
                        if j == 0:
                            wait(dve, "h_ready", b["h_ready"] + nt * g)
                        dve.tensor_tensor(m[:, j % 2, :], silu[:, j % 2, :], bU[j % 2][:, :], ALU.mult).then_inc(S["m_ready"], 1)
                        wait(dve, "m_ready", b["m_ready"] + t + 1)
                        wait(dve, "gx_ready", b["gx_ready"] + t + 1)
                        wait_slot(dve, "hlo_ready", b, nt, g, j, FRING)
                        dve.tensor_tensor(h[:, j % FRING, :], m[:, j % 2, :], bG[j % 2][:, :], ALU.mult).then_inc(S["h_ready"], 1)
                        if j == 3 and not is_first(g):
                            x_update(b, g - 1)
                        if not is_last(g):
                            if j == 0:
                                ln_stats(b, g + 1)
                            if j == 1:
                                ln_apply(b, g + 1)
                            if j == 5:
                                x_lo(b, g + 1)
                            if j == 7:
                                route_begin(b, g + 1, kind)
                            if j == 8:
                                route_end(b, g + 1, kind)
                for g in range(NG):
                    wait(dve, "x_updated", b["x_updated"])
                    if b["x_updated"] == 0:
                        dve.wait_ge(x_loaded[g], 16)
                ln_stats(b, 0)
                ln_apply(b, 0)
                x_lo(b, 0)
                route_begin(b, 0, kind)
                route_end(b, 0, kind)
                groups(nc.vector, group, ch, per)
                x_update(b, NG - 1)

            def mamba(b):
                def prepare():
                    dve.wait_ge(mamba_loaded, ALL_MLOADS)
                    for n in range(2):
                        ch.add(dve.memset(xm[n][:, :, 0:PAD], 0.0))
                        ch.add(dve.tensor_scalar(w3g[:, n, :], w3[:, n, :], lng[:, n:n + 1], None, ALU.mult))
                    dve.tensor_copy(lnbw[:, :, :], lnb[:, :].unsqueeze(2).broadcast_to([P, 2, P])).then_inc(mprep_dve, 1)
                    for k in range(TAPS):
                        dve.wait_ge(wchi_ready, k + 1)
                        ch.add(dve.scalar_tensor_tensor(wc[1][:, k, :], [bA[0], bA[1], bU[0], bU[1]][k][:, 0:CH], CS, wc[0][:, k, :],
                                                        ALU.mult, ALU.subtract))
                    dve.wait_ge(wchi_ready, TAPS + 1)
                    ch.add(dve.scalar_tensor_tensor(wdts[:, 1, :], wdt[:, :], CS, wdts[:, 0, :], ALU.mult, ALU.subtract))
                    dve.wait_ge(mprep_act, 3)
                    ch.join()
                    dve.scalar_tensor_tensor(win2s[:, 1, :], win2[:, :], CS, win2s[:, 0, :], ALU.mult, ALU.subtract).then_inc(mprep_dve, 1)

                def g_mask(g):
                    for q in range(2):
                        wait(dve, "g_ready", b["g_ready"] + 2 * g + q + 1)
                        src = mG[q][:, 0:4 * P].rearrange("p (t c) -> p t c", t=2)[:, :, 0:P]
                        dve.tensor_tensor(gm[:, 2 * q:2 * q + 2, :], src, tri[:, :].unsqueeze(1).broadcast_to([P, 2, P]),
                                          ALU.mult).then_inc(S["gm_ready"], 1)

                def mixers(g):
                    wait(dve, "gm_ready", b["gm_ready"] + 2 * g + 2)
                    wait(dve, "yd_ready", b["yd_ready"] + 2 * g)
                    for t in range(GT):
                        wait(dve, "decay_ready", b["decay_ready"] + GT * g + t + 1)
                        dve.tensor_tensor(mt[:, t, :].rearrange("p (h l) -> p h l", l=P), decay[:, t, :].rearrange("p (h l) -> p h l", l=P),
                                          gm[:, t, :].unsqueeze(1).broadcast_to([P, HEADS, P]), ALU.mult).then_inc(S["mt_ready"], 1)

                def x_lo_pair(g):
                    wait(dve, "xhi_ready", b["xhi_ready"] + g + 1)
                    dve.tensor_tensor(pair(xm[1]), bT[:, :].rearrange("p (q s) -> p q s", q=2), pair(xm[0]),
                                      ALU.subtract).then_inc(S["xlo_ready"], 1)

                def dt_clip(g):
                    wait(dve, "dt_ready", b["dt_ready"] + g + 1)
                    src = bT[:, 0:GT * HEADS].rearrange("p (t h) -> p t h", t=GT)
                    ch.link(dve.tensor_scalar(dt[:, :, :], src, 1.0 / CS, None, ALU.mult))
                    ch.add(dve.tensor_scalar(dtx[:, :, :], dt[:, :, :], 20.0, 0.0, ALU.subtract, ALU.max))
                    dve.tensor_scalar(dtc[:, :, :], dt[:, :, :], 20.0, None, ALU.min).then_inc(S["dtc_ready"], 1)

                def dt_rate(g):
                    ch.join()
                    wait(dve, "sp_ready", b["sp_ready"] + g + 1)
                    ch.link(dve.tensor_tensor(dt[:, :, :], sp[:, :, :], dtx[:, :, :], ALU.add))
                    wait(dve, "cum_ready", b["cum_ready"] + g)
                    wait(dve, "trid_ready", b["trid_ready"] + GT * g)
                    dve.tensor_tensor(dd[:, :, :], dt[:, :, :], rate[:, :].unsqueeze(1).broadcast_to([P, GT, HEADS]),
                                      ALU.mult).then_inc(S["d_ready"], 1)

                def mix(g):
                    wait(dve, "yoff_ready", b["yoff_ready"] + g + 1)
                    wait(dve, "gelu_ready", b["gelu_ready"] + 2 * g + 2)
                    ch.link(dve.tensor_tensor(yo[:, :, :].rearrange("p q (h d) -> p q h d", d=HD),
                                              mY[:, :].rearrange("p (q h d) -> p q h d", q=2, h=HEADS),
                                              ed[:, 1, :, :].unsqueeze(3).broadcast_to([P, 2, HEADS, HD]), ALU.mult))
                    for q in range(2):
                        ch.add(dve.tensor_tensor(yo[:, q, :], mU[q][:, INNER:2 * INNER], yo[:, q, :], ALU.add))
                        ch.add(dve.tensor_tensor(hm[:, 2 * q, :], mU[q][:, 0:INNER], u2[:, 2 * q, :], ALU.mult))
                    ch.join()
                    odd = hm[:, :, :].rearrange("p (q t) c -> p q t c", t=2)[:, :, 1, :]
                    dve.tensor_tensor(odd, yo[:, :, :], u2[:, :, :].rearrange("p (q t) c -> p q t c", t=2)[:, :, 1, :],
                                      ALU.mult).then_inc(S["mixed"], 1)

                def hidden_norm(g):
                    wait(dve, "mixed", b["mixed"] + g + 1)
                    for t in range(GT):
                        ch.add(dve.bn_stats(hstats[:, t, :], hm[:, t, :]))
                    ch.join()
                    for t in range(GT):
                        ins = dve.bn_aggr(hmv[:, t, :], hstats[:, t, :])
                        if t < GT - 1:
                            ch.add(ins)
                        else:
                            ins.then_inc(S["hvar_ready"], 1)

                def hidden_apply(g):
                    ch.join()
                    wait(dve, "hrstd_ready", b["hrstd_ready"] + g + 1)
                    wait(dve, "hnT_ready", b["hnT_ready"] + 2 * g)
                    for t in range(GT):
                        ins = dve.tensor_scalar(hn[:, t, :], hm[:, t, :], hmv[:, t, 0:1], hrstd[:, t:t + 1], ALU.subtract, ALU.mult)
                        if t < GT - 1:
                            ch.add(ins)
                        else:
                            ins.then_inc(S["hn_ready"], 1)

                def prelu(dst, src, neg, name):
                    n = src.shape[0]
                    ch.link(dve.tensor_scalar(neg, src, 0.0, slope[0:n, 0:1], ALU.min, ALU.mult))
                    dve.scalar_tensor_tensor(dst, src, 0.0, neg, ALU.max, ALU.add).then_inc(S[name], 1)

                def x_conv(g):
                    for n in range(2):
                        wait(dve, "convx_ready", b["convx_ready"] + 2 * g + n + 1)
                        dve.scalar_tensor_tensor(xc[:, 2 * n:2 * n + 2, :], mX[n][:, :].rearrange("p (t c) -> p t c", t=2), 1.0 / CS,
                                                 xbias[:, :].unsqueeze(1).broadcast_to([P, 2, INNER]), ALU.mult, ALU.add)\
                           .then_inc(S["xc_biased"], 1)
                    wait(dve, "xc_biased", b["xc_biased"] + 2 * g + 2)
                    wait(dve, "yd_ready", b["yd_ready"] + 2 * g)
                    wait(dve, "xs_ready", b["xs_ready"] + g)
                    prelu(xv[:, :, :].rearrange("p t c -> p (t c)"), xc[:, :, :].rearrange("p t c -> p (t c)"),
                          xneg[:, :, :].rearrange("p t c -> p (t c)"), "xs_val")

                def bc_conv(g):
                    for n in range(2):
                        wait(dve, "bc_biased", b["bc_biased"] + 2 * g + n + 1)
                        wait(dve, "g_ready", b["g_ready"] + 2 * g)
                        prelu(bcv[:, n, :], bcc[:, n, :], bcneg[:, n, :], "bc_val")

                def hnT_copy(g):
                    wait(dve, "hnT_ready", b["hnT_ready"] + 2 * g + 2)
                    wait(dve, "y_ready", b["y_ready"] + g)
                    dve.tensor_copy(hnT[:, 1, :], bT[:, :]).then_inc(S["hnT1_copied"], 1)

                def x_update(g):
                    wait(dve, "y_ready", b["y_ready"] + g + 1)
                    wait(dve, "x_biased", b["x_biased"] + g + 1)
                    dst = x[:, bass.ts(g, GT), :]
                    dve.tensor_tensor(dst, dst, mY[:, :].rearrange("p (t d) -> p t d", d=P), ALU.add).then_inc(S["x_updated"], 1)

                def body(g):
                    nxt = not is_last(g)
                    if nxt:
                        ln_stats(b, g + 1)
                        ln_apply(b, g + 1)
                    g_mask(g)
                    mixers(g)
                    if nxt:
                        x_lo_pair(g + 1)
                        dt_clip(g + 1)
                    mix(g)
                    hidden_norm(g)
                    if nxt:
                        dt_rate(g + 1)
                    hidden_apply(g)
                    if nxt:
                        x_conv(g + 1)
                        bc_conv(g + 1)
                    hnT_copy(g)
                    x_update(g)
                prepare()
                if b["x_updated"] == 0:
                    for g in range(NG):
                        dve.wait_ge(x_loaded[g], 16)
                wait(dve, "x_updated", b["x_updated"])
                ln_stats(b, 0)
                ln_apply(b, 0)
                x_lo_pair(0)
                dt_clip(0)
                dt_rate(0)
                x_conv(0)
                bc_conv(0)
                with nc.vector.Fori(0, NG - 1) as g:
                    body(g)
                body(NG - 1)

            def attention(b):
                def prepare():
                    dve.wait_ge(aprep_act, 2)
                    dve.scalar_tensor_tensor(wqks[:, 1, :], wqk[:, :], WSCALE, wqks[:, 0, :], ALU.mult, ALU.subtract).then_inc(aprep_dve, 1)
                    dve.scalar_tensor_tensor(wvs[:, 1, :], wv[:, :], WSCALE, wvs[:, 0, :], ALU.mult, ALU.subtract).then_inc(aprep_dve, 1)
                    ones = va[:, :, :, :].rearrange("p a t (h e) -> p (a t h) e", e=AD + 1)[:, :, AD:AD + 1]
                    dve.memset(ones, 1.0).then_inc(aprep_dve, 1)

                def x_lo_pair(g):
                    wait(dve, "xhi_ready", b["xhi_ready"] + g + 1)
                    dve.tensor_tensor(xa[1][:, :], bT[:, :], xa[0][:, :], ALU.subtract).then_inc(S["xlo_ready"], 1)

                def rope_mul(q, n):
                    t = 2 * q.value + n
                    wait(dve, "qk_ready", b["qk_ready"] + t + 1)
                    if q.index >= 1:
                        wait(dve, "roped", b["roped"] + t - 1)
                    for k, table in enumerate((ropec, ropes)):
                        ins = dve.scalar_tensor_tensor(rope[:, n, k, :], bT[:, k * SEQ:(k + 1) * SEQ], 1.0 / WSCALE, table[:, :], ALU.mult, ALU.mult)
                    ins.then_inc(S["rope_mul"], 1)

                def unit_max(q, u):
                    wait(dve, "s1_ready", b["s1_ready"] + NU * q.value + u + 1)
                    dve.tensor_reduce(mx[:, u // 2, (u % 2) * 8:(u % 2) * 8 + 8], sets[(2 * u + 1) % 3][:, :].rearrange("p (h k) -> p h k", k=P),
                                      AX, ALU.max).then_inc(S["max_ready"], 1)

                def negate(q):
                    wait(dve, "max_ready", b["max_ready"] + NU * q.value + NU)
                    ch.link(dve.tensor_tensor(mx[:, 1, :], mx[:, 1, :], mx[:, 2, :], ALU.max))
                    ch.link(dve.tensor_scalar(negm[:, :, :], mx[:, 0:2, :], -1.0, None, ALU.mult))
                    wait(dve, "mT_ready", b["mT_ready"] + q.value)
                    ch.link(dve.tensor_copy(mparts[:, :, 0:AH], negm[:, :, :]))
                    dve.tensor_tensor(mparts[:, :, AH:2 * AH], negm[:, :, :], mparts[:, :, 0:AH], ALU.subtract).then_inc(S["negmax"], 1)

                def normalise(q):
                    wait(dve, "pv_done", b["pv_done"] + NU * (q.value + 1))
                    o = bO[:, 0:2 * AH * (AD + 1)].rearrange("p (t h e) -> p t h e", t=2, e=AD + 1)
                    ch.link(dve.reciprocal(orec[:, :, :], o[:, :, :, AD]))
                    wait(dve, "oTa_ready", b["oTa_ready"] + q.value)
                    dve.tensor_tensor(on[:, :, :].rearrange("p t (h e) -> p t h e", e=AD), o[:, :, :, 0:AD],
                                      orec[:, :, :].unsqueeze(3).broadcast_to([P, 2, AH, AD]), ALU.mult).then_inc(S["onorm"], 1)

                def x_update(q):
                    wait(dve, "ya_ready", b["ya_ready"] + q.value + 1)
                    wait(dve, "x_biased", b["x_biased"] + q.half + 1)
                    dst = x[:, bass.ts(q.value, 2), :]
                    dve.tensor_tensor(dst, dst, bT[:, 0:2 * P].rearrange("p (t d) -> p t d", d=P), ALU.add).then_inc(S["x_updated"], 1)

                def step(q):
                    front, back = q.index < NSEQ - 2, q.index < NSEQ - 1
                    if front and q.parity == 0:
                        ln_stats(b, q.half + 1)
                        ln_apply(b, q.half + 1)
                    for u in range(NU):
                        if back:
                            unit_max(q.plus(1), u)
                        if front:
                            if u == 0 and q.parity == 0:
                                x_lo_pair(q.half + 1)
                            if u == 2:
                                rope_mul(q.plus(2), 0)
                            if u == 3:
                                rope_mul(q.plus(2), 1)
                    if back:
                        negate(q.plus(1))
                    normalise(q)
                    x_update(q)
                if b["x_updated"] == 0:
                    for g in range(NG):
                        dve.wait_ge(x_loaded[g], 16)
                wait(dve, "x_updated", b["x_updated"])
                prepare()
                ln_stats(b, 0)
                ln_apply(b, 0)
                x_lo_pair(0)
                for q in (Seq(0), Seq(1)):
                    for n in range(2):
                        rope_mul(q, n)
                for u in range(NU):
                    unit_max(Seq(0), u)
                negate(Seq(0))
                steps(nc.vector, step)
            dve.wait_ge(consts_loaded, ALL_CONSTS)
            for ph, b in zip(phases, base):
                {"M": mamba, "A": attention}[ph](b) if ph in "MA" else layer(ph, b, {"F0": 31, "F1": 31}[ph])

        @block.tensor
        def _(pe):
            def split_product(out, w, wcols, rhs_hi, rhs_lo, start=True, stop=True):
                nc.tensor.matmul(out, w[0][:, wcols], rhs_hi, start=start, stop=False)
                nc.tensor.matmul(out, w[0][:, wcols], rhs_lo, start=False, stop=False)
                return nc.tensor.matmul(out, w[1][:, wcols], rhs_hi, start=False, stop=stop)

            def xn_transpose(b, g):
                wait(pe, "xn_ready", b["xn_ready"] + g + 1)
                for i in range(GT):
                    ins = nc.tensor.transpose(bT[:, i * P:(i + 1) * P], xn[:, i, :], ident[:, :])
                ins.then_inc(S["xnT_ready"], 1)

            def logits(b, g, k):
                n = (E0, E1)[k]
                wait(pe, "xlo_ready", b["xlo_ready"] + g + 1)
                for i in range(GT):
                    tok = bass.ds(g * GROUP + i * P, P)
                    o = bT[:, i * n:(i + 1) * n]
                    nc.tensor.matmul(o, xhi[:, tok], wrs[k][:, 0, :], start=i == 0, stop=False, skip_group_check=True)
                    nc.tensor.matmul(o, xhi[:, tok], wrs[k][:, 1, :], start=False, stop=False, skip_group_check=True)
                    ins = nc.tensor.matmul(o, xlo[:, tok], wrs[k][:, 0, :], start=False, stop=True, skip_group_check=True)
                ins.then_inc(S["logits_ready"], 1)

            def gates_transpose(b, g, kg):
                wait_apart(pe, "gates_ready", b["gates_ready"] + g + 1)
                for i in range(GT):
                    ins = nc.tensor.transpose(bTb[:, i * P:(i + 1) * P], gparts[:, i, :], identb[:, :])
                ins.then_inc(S["gatesT_ready"], 1)

            def out_transpose(b, g):
                wait(pe, "o_copied", b["o_copied"] + g + 1)
                for i in range(GT):
                    ins = nc.tensor.transpose(bT[:, i * P:(i + 1) * P], oT[:, i * P:(i + 1) * P], ident[:, :])
                ins.then_inc(S["outT_ready"], 1)

            def layer(kind, b):
                k = 0 if kind == "F0" else 1
                nt, kg = NT[kind], 3 * (E0 if k == 0 else E1 + 1)

                def up(g, j):
                    cols = slice(j * P, (j + 1) * P)
                    hi, lo = xhi[:, bass.ts(g, GROUP)], xlo[:, bass.ts(g, GROUP)]
                    wait_slot(pe, "silu_ready", b, nt, g, j, 2)
                    split_product(bA[j % 2][:, :], W["w1g", k], cols, hi, lo).then_inc(S["a_ready"], 1)
                    wait_slot(pe, "m_ready", b, nt, g, j, 2)
                    split_product(bU[j % 2][:, :], W["w1u", k], cols, hi, lo).then_inc(S["u_ready"], 1)
                    wait_slot(pe, "h_ready", b, nt, g, j, 2)
                    nc.tensor.matmul(bG[j % 2][:, :], sel[k][:, cols], gT[:, bass.ts(g, GROUP)],
                                     start=True, stop=True).then_inc(S["gx_ready"], 1)

                def down(g, j):
                    r = j % HRING
                    wait(pe, "hlo_ready", b["hlo_ready"] + nt * g + j + 1)
                    if j == 0:
                        wait(pe, "o_copied", b["o_copied"] + g)
                    split_product(bO[:, :], W["w2", k], slice(j * P, (j + 1) * P), hhi[:, r, :], hlo[:, r, :],
                                  start=j == 0, stop=j == nt - 1).then_inc(S["h_used"], 1)

                def group(g):
                    for j in range(nt):
                        up(g, j)
                        if j >= LAG:
                            down(g, j - LAG)
                        elif not is_first(g):
                            down(g - 1, nt + j - LAG)
                        if j == 3 and not is_first(g):
                            out_transpose(b, g - 1)
                        if not is_last(g):
                            if j == 4:
                                if not is_first(g):
                                    wait(pe, "x_updated", b["x_updated"] + g)
                                xn_transpose(b, g + 1)
                            if j == 6:
                                logits(b, g + 1, k)
                            if j == 9:
                                gates_transpose(b, g + 1, kg)
                            if j == nt - 1:
                                wait(pe, "gT_ready", b["gT_ready"] + g + 2)
                xn_transpose(b, 0)
                logits(b, 0, k)
                gates_transpose(b, 0, kg)
                wait(pe, "gT_ready", b["gT_ready"] + 1)
                groups(nc.tensor, group)
                for j in range(nt - LAG, nt):
                    down(NG - 1, j)
                out_transpose(b, NG - 1)
            pe.wait_ge(consts_loaded, ALL_CONSTS)
            pe.wait_ge(idents_loaded, 32)
            pe.wait_ge(wlo_ready, len(WEIGHTS) + 2)

            def mamba(b):
                def prepare():
                    pe.wait_ge(mamba_loaded, ALL_MLOADS)
                    wait(pe, "x_updated", b["x_updated"])
                    for k in range(TAPS):
                        for c in range(CH // P):
                            ins = nc.tensor.matmul([bA[0], bA[1], bU[0], bU[1]][k][:, 0:CH], win1[:, c, :], convw[:, c, k, :],
                                                   start=c == 0, stop=c == CH // P - 1)
                        ins.then_inc(wc_ready, 1)
                    pe.wait_ge(mprep_dve, 1)
                    for k in range(2):
                        ins = nc.tensor.matmul(bT[:, 0:P], lnbw[:, k, :], w3[:, k, :], start=k == 0, stop=k == 1)
                    ins.then_inc(wc_ready, 1)
                    pe.wait_ge(mprep_act, 2)
                    pe.wait_ge(mprep_dve, 2)

                def taps(out, lhs, rhs):
                    for k in range(TAPS):
                        for n, (p, q) in enumerate(((0, 0), (0, 1), (1, 0))):
                            ins = nc.tensor.matmul(out, lhs(p, k), rhs(q, k), start=k == 0 and n == 0, stop=k == TAPS - 1 and n == 2)
                    return ins

                def tile_of(part, t, k):
                    at = PAD - (TAPS - 1) + k + (t % 2) * P
                    return xm[part][:, t // 2, at:at + P]

                def seg(g):
                    wait(pe, "gelu_ready", b["gelu_ready"] + 2 * g + 2)
                    wait(pe, "bc_biased", b["bc_biased"] + 2 * g + 2)
                    for t in range(GT):
                        wait(pe, "trid_ready", b["trid_ready"] + GT * g + t + 1)
                        nc.tensor.matmul(mSeg[t][:, :], later[:, :], trid[:, t, :], start=True, stop=True).then_inc(S["seg_ready"], 1)
                    wait(pe, "x_updated", b["x_updated"] + g)
                    for n, m_ in ((0, later), (1, tri)):
                        ins = nc.tensor.matmul(mCum[:, n * 2 * HEADS:(n + 1) * 2 * HEADS].rearrange("p (q h) -> p q h", q=2), m_[:, :],
                                               dd[:, :, :].rearrange("p (q t) h -> p q t h", t=2)[:, :, n, :],
                                               start=n == 0, stop=True, skip_group_check=True)
                    ins.then_inc(S["cum_ready"], 1)

                def g_blocks(g):
                    wait(pe, "bc_val", b["bc_val"] + 2 * g + 2)
                    wait(pe, "xc_biased", b["xc_biased"] + 2 * g + 2)
                    for q in range(2):
                        o = q * SEQ
                        nc.tensor.matmul(mG[q][:, 0:SEQ], bcv[:, 0, o:o + P], bcv[:, 1, o:o + SEQ], start=True, stop=True)
                        nc.tensor.matmul(mG[q][:, SEQ:SEQ + P], bcv[:, 0, o + P:o + SEQ], bcv[:, 1, o + P:o + SEQ],
                                         start=True, stop=True).then_inc(S["g_ready"], 1)

                def dt_project(g):
                    wait(pe, "xlo_ready", b["xlo_ready"] + g + 1)
                    for t in range(GT):
                        o = bT[:, t * HEADS:(t + 1) * HEADS]
                        for n, (p, q) in enumerate(((0, 0), (0, 1), (1, 0))):
                            ins = nc.tensor.matmul(o, tile_of(p, t, TAPS - 1), wdts[:, q, :], start=t == 0 and n == 0, stop=n == 2,
                                                   skip_group_check=True)
                    ins.then_inc(S["dt_ready"], 1)

                def y_products(g):
                    wait(pe, "xs_val", b["xs_val"] + g + 1)
                    for t in range(GT):
                        wait(pe, "mt_ready", b["mt_ready"] + GT * g + t + 1)
                        for hd in range(HEADS):
                            o = (t % 2) * INNER + hd * HD
                            ins = nc.tensor.matmul(mU[t // 2][:, o:o + HD], mt[:, t, hd * P:(hd + 1) * P], xv[:, t, hd * HD:(hd + 1) * HD],
                                                   start=True, stop=True)
                        if t % 2:
                            ins.then_inc(S["yd_ready"], 1)
                    wait(pe, "goff_ready", b["goff_ready"] + 2 * g + 2)
                    wait(pe, "xs_ready", b["xs_ready"] + g + 1)
                    for q in range(2):
                        ins = nc.tensor.matmul(mY[:, q * INNER:(q + 1) * INNER], goff[:, q, :], xsd[:, q, :], start=True, stop=True)
                    ins.then_inc(S["yoff_ready"], 1)

                def convolve(g):
                    wait(pe, "goff_ready", b["goff_ready"] + 2 * g)
                    for n in range(2):
                        for t in (2 * n, 2 * n + 1):
                            ins = taps(mX[n][:, (t % 2) * INNER:(t % 2 + 1) * INNER], lambda p, k: tile_of(p, t, k),
                                       lambda q, k: wc[q][:, k, 0:INNER])
                        ins.then_inc(S["convx_ready"], 1)
                    wait(pe, "decay_ready", b["decay_ready"] + GT * g)
                    for n, (bk, s) in enumerate(((mB, "convb_ready"), (mC, "convc_ready"))):
                        c = INNER + n * STATE
                        taps(bk[0:STATE, :].rearrange("p (q s) -> p q s", q=2), lambda p, k: wc[p][:, k, c:c + STATE],
                             lambda q, k: xm[q][:, :, PAD - (TAPS - 1) + k:PAD - (TAPS - 1) + k + SEQ]).then_inc(S[s], 1)
                    wait(pe, "mixed", b["mixed"] + g)
                    for t in range(GT):
                        for n, (p, q) in enumerate(((0, 0), (0, 1), (1, 0))):
                            ins = nc.tensor.matmul(mU[t // 2][:, (t % 2) * INNER:(t % 2 + 1) * INNER], tile_of(p, t, TAPS - 1), win2s[:, q, :],
                                                   start=n == 0, stop=n == 2)
                        if t % 2:
                            ins.then_inc(S["u2_ready"], 1)

                def out_product(g):
                    wait(pe, "hn_ready", b["hn_ready"] + g + 1)
                    if not is_last(g):
                        wait(pe, "dtc_ready", b["dtc_ready"] + g + 2)
                    for k, bk in enumerate((mY, bT)):
                        for t in range(GT):
                            ins = nc.tensor.transpose(bk[:, t * P:(t + 1) * P], hn[:, t, k * P:(k + 1) * P], ident[:, :])
                        ins.then_inc(S["hnT_ready"], 1)
                    wait(pe, "hnT0_copied", b["hnT0_copied"] + g + 1)
                    wait(pe, "hnT1_copied", b["hnT1_copied"] + g + 1)
                    for t in range(GT):
                        for k in range(2):
                            ins = nc.tensor.matmul(mY[:, t * P:(t + 1) * P], hnT[:, k, t * P:(t + 1) * P], w3g[:, k, :],
                                                   start=k == 0, stop=k == 1)
                    ins.then_inc(S["y_ready"], 1)

                def body(g):
                    nxt = not is_last(g)
                    seg(g)
                    g_blocks(g)
                    if nxt:
                        wait(pe, "hnT1_copied", b["hnT1_copied"] + g)
                        xn_transpose(b, g + 1)
                        dt_project(g + 1)
                    y_products(g)
                    if nxt:
                        convolve(g + 1)
                    out_product(g)
                prepare()
                xn_transpose(b, 0)
                dt_project(0)
                convolve(0)
                with nc.tensor.Fori(0, NG - 1) as g:
                    body(g)
                body(NG - 1)

            def attention(b):
                def project(q, n):
                    cols = slice(q.parity * SEQ, (q.parity + 1) * SEQ)
                    for k in range(2):
                        c = slice((2 * n + k) * P, (2 * n + k + 1) * P)
                        o = bT[:, k * SEQ:(k + 1) * SEQ]
                        nc.tensor.matmul(o, wqks[:, 0, c], xa[0][:, cols], start=True, stop=False)
                        nc.tensor.matmul(o, wqks[:, 0, c], xa[1][:, cols], start=False, stop=False)
                        ins = nc.tensor.matmul(o, wqks[:, 1, c], xa[0][:, cols], start=False, stop=True)
                    ins.then_inc(S["qk_ready"], 1)

                def values(q):
                    for t in range(2):
                        cols = slice(q.parity * SEQ + t * P, q.parity * SEQ + (t + 1) * P)
                        o = bT[:, t * P:(t + 1) * P]
                        nc.tensor.matmul(o, xa[0][:, cols], wvs[:, 0, :], start=True, stop=False)
                        nc.tensor.matmul(o, xa[1][:, cols], wvs[:, 0, :], start=False, stop=False)
                        ins = nc.tensor.matmul(o, xa[0][:, cols], wvs[:, 1, :], start=False, stop=True)
                    ins.then_inc(S["v_ready"], 1)

                def scores(dst, u, mask, lhs, rhs, rows, name):
                    qt, kt = UNITS[u // 2]
                    for ii in range(2):
                        if qt == kt:
                            nc.tensor.matmul(dst[:, ii * 512:(ii + 1) * 512], identb[:, :], mask[:, :], start=True, stop=False,
                                             skip_group_check=True)
                    for j in range(4):
                        for ii in range(2):
                            r = 32 * (2 * (u % 2) + ii)
                            ins = nc.tensor.matmul(dst[:, (4 * ii + j) * P:(4 * ii + j + 1) * P],
                                                   lhs[0][r:r + rows, j, lhs[1] * P:(lhs[1] + 1) * P],
                                                   rhs[0][r:r + rows, j, rhs[1] * P:(rhs[1] + 1) * P],
                                                   start=qt != kt, stop=True, skip_group_check=True)
                    ins.then_inc(S[name], 1)

                def first_pass(q, u):
                    qt, kt = UNITS[u // 2]
                    if u == 0:
                        pe.wait_ge(spread_done[q.parity], SPREAD * (q.half + 1))
                    scores(sets[(2 * u + 1) % 3], u, maskq, (qa[q.parity], qt), (ka[q.parity], kt), ROWS, "s1_ready")

                def second_pass(q, u):
                    qt, kt = UNITS[u // 2]
                    if u == 0:
                        pe.wait_ge(maxima_done, MAXIMA * (q.value + 1))
                    scores(sets[2 * u % 3], u, maskk, (ka[q.parity], kt), (qa[q.parity], qt), 32, "s2_ready")

                def weighted(q, u):
                    qt, kt = UNITS[u // 2]
                    wait(pe, "exp_ready", b["exp_ready"] + NU * q.value + u + 1)
                    if u == 0:
                        wait(pe, "onorm", b["onorm"] + q.value)
                        wait(pe, "v_copied", b["v_copied"] + q.value + 1)
                    w = AD + 1
                    for hh in range(8):
                        hd = 8 * (u % 2) + hh
                        ins = nc.tensor.matmul(bO[:, (qt * AH + hd) * w:(qt * AH + hd + 1) * w], pt[:, u % PRING, hh * P:(hh + 1) * P],
                                               va[:, q.parity, kt, hd * w:(hd + 1) * w], start=u == 0 and hh == 0, stop=True,
                                               skip_group_check=True)
                    ins.then_inc(S["pv_done"], 1)

                def maxima_transpose(q):
                    wait_apart(pe, "negmax", b["negmax"] + q.value + 1)
                    for j in range(4):
                        for t in range(2):
                            ins = nc.tensor.transpose(bTh[0:8, (2 * j + t) * P:(2 * j + t + 1) * P], mparts[:, t, j::4], identh[:, :])
                    ins.then_inc(S["mT_ready"], 1)

                def out_product(q):
                    wait(pe, "onorm", b["onorm"] + q.value + 1)
                    for t in range(2):
                        ins = nc.tensor.transpose(bT[:, t * P:(t + 1) * P], on[:, t, :], ident[:, :])
                    ins.then_inc(S["oTa_ready"], 1)
                    wait(pe, "oTa_copied", b["oTa_copied"] + q.value + 1)
                    for t in range(2):
                        ins = nc.tensor.matmul(bT[:, t * P:(t + 1) * P], oTa[:, t * P:(t + 1) * P], wo[:, :], start=True, stop=True)
                    ins.then_inc(S["ya_ready"], 1)

                def step(q):
                    front, back = q.index < NSEQ - 2, q.index < NSEQ - 1
                    for u in range(NU):
                        if back or u < 2:
                            wait(pe, "max_ready", b["max_ready"] + NU * q.value + NU + u - 1)
                        second_pass(q, u)
                        if back:
                            if u or q.index:
                                wait(pe, "exp_ready", b["exp_ready"] + NU * q.value + u)
                            first_pass(q.plus(1), u)
                        if u:
                            weighted(q, u - 1)
                        if front:
                            n = q.plus(2)
                            if u == 0 and q.parity == 0:
                                if q.index:
                                    wait(pe, "x_updated", b["x_updated"] + q.value)
                                xn_transpose(b, n.half)
                            if u == 1:
                                if q.parity:
                                    wait(pe, "x_updated", b["x_updated"] + q.value)
                                else:
                                    wait(pe, "xlo_ready", b["xlo_ready"] + n.half + 1)
                                project(n, 0)
                            if u == 2:
                                wait(pe, "rope_mul", b["rope_mul"] + 2 * n.value + 1)
                                project(n, 1)
                    weighted(q, NU - 1)
                    if front:
                        wait(pe, "rope_mul", b["rope_mul"] + 2 * n.value + 2)
                        values(n)
                        wait(pe, "v_copied", b["v_copied"] + n.value + 1)
                    if back:
                        maxima_transpose(q.plus(1))
                        wait(pe, "mrow_ready", b["mrow_ready"] + q.value + 2)
                    out_product(q)
                wait(pe, "x_updated", b["x_updated"])
                pe.wait_ge(aprep_dve, 3)
                xn_transpose(b, 0)
                wait(pe, "xlo_ready", b["xlo_ready"] + 1)
                for q in (Seq(0), Seq(1)):
                    for n in range(2):
                        if n or q.value:
                            wait(pe, "rope_mul", b["rope_mul"] + 2 * q.value + n)
                            wait(pe, "v_copied", b["v_copied"] + q.value)
                        project(q, n)
                    wait(pe, "rope_mul", b["rope_mul"] + 2 * q.value + 2)
                    values(q)
                for u in range(NU):
                    if u > 2:
                        wait(pe, "max_ready", b["max_ready"] + u - 2)
                    first_pass(Seq(0), u)
                wait(pe, "v_copied", b["v_copied"] + 2)
                maxima_transpose(Seq(0))
                wait(pe, "mrow_ready", b["mrow_ready"] + 1)
                steps(nc.tensor, step)
            for ph, b in zip(phases, base):
                {"M": mamba, "A": attention}[ph](b) if ph in "MA" else layer(ph, b)


_CONSTS = {}


def kernel(_phases=("F0", "M", "F0", "F1", "A", "F1"), **inputs):
    import numpy as np
    import ml_dtypes
    import concourse.bacc as _bacc
    from concourse.bass_utils import run_bass_kernel_spmd as _run

    def cat(*a):
        return np.concatenate(a, axis=0)

    a = {k: np.asarray(v) for k, v in inputs.items()}
    experts_in = lambda w, s: cat(a[w], a[s][None])
    cols = lambda w: np.transpose(w.reshape(-1, w.shape[-1]), (1, 0))
    rows = lambda w: np.transpose(w.reshape(-1, P, P), (1, 0, 2)).reshape(P, -1)
    arrays = {
        "x": a["L0_attn_u"],
        "w1g0": np.transpose(a["L0_ffn_W1"], (1, 0, 2)).reshape(P, -1),
        "w1u0": np.transpose(a["L0_ffn_W3"], (1, 0, 2)).reshape(P, -1),
        "w20": rows(a["L0_ffn_W2"]),
        "w1g1": cols(experts_in("L1_ffn_Wg", "L1_ffn_Wg_s")),
        "w1u1": cols(experts_in("L1_ffn_Wu", "L1_ffn_Wu_s")),
        "w21": rows(np.transpose(experts_in("L1_ffn_Wd", "L1_ffn_Wd_s"), (0, 2, 1))),
        "wr0": a["L0_ffn_Wg"].T, "wr1": a["L1_ffn_Wr"].T, "rb": a["L1_ffn_rb"],
    }
    bf = ml_dtypes.bfloat16
    w_in, conv = a["L0_attn_W_in1"], a["L0_attn_conv_w"]
    taps_in = np.transpose(conv, (1, 2, 0)).reshape(CH // P, P, TAPS, CH)
    arrays.update({
        "win1": np.transpose(w_in[INNER:INNER + CH].reshape(CH // P, P, P), (1, 0, 2)),
        "convw": np.transpose(taps_in, (1, 0, 2, 3)),
        "wdt": w_in[INNER + CH:].T, "win2": a["L0_attn_W_in2"].T,
        "w3": np.transpose(a["L0_attn_W_in3"].T.reshape(2, P, P), (1, 0, 2)),
        "lng": a["L0_attn_ln_g"].reshape(2, P).T, "lnb": a["L0_attn_ln_b"].reshape(2, P).T,
        "xbias": a["L0_attn_conv_b"][:INNER], "bcbias": a["L0_attn_conv_b"][INNER:].reshape(2, STATE).T,
        "slope": a["L0_attn_prelu_a"].reshape(1), "alog": a["L0_attn_A_log"],
    })
    partner = np.roll(np.arange(P), P // 2)
    wq, wk = a["L1_attn_wq"], a["L1_attn_wk"]
    arrays.update({"wqk": np.transpose(cat(wq, wq[partner], wk, wk[partner])), "wv": a["L1_attn_wv"].T,
                   "wo": a["L1_attn_out_w"].T, "obias": a["L1_attn_out_b"]})
    half = P // 2
    freqs = np.float32(1.0) / np.float32(10000.0) ** (np.arange(half, dtype=np.float32) / np.float32(half))
    ang = np.arange(SEQ, dtype=np.float32)[None, :] * freqs[:, None].astype(np.float32)
    arrays["ropec"] = np.tile(np.cos(ang), (2, 1)).astype(np.float32)
    arrays["ropes"] = cat(-np.sin(ang), np.sin(ang)).astype(np.float32)
    slopes = 2.0 ** (-8.0 * (np.arange(AH) + 1) / AH) * AD ** 0.5
    pos = np.arange(SEQ, dtype=np.float64)
    qinit, kinit = np.zeros((4, 32, 4, SEQ), np.float16), np.zeros((4, 32, 4, SEQ), np.float16)
    for n, v in enumerate((slopes[:, None] + 0 * pos, -slopes[:, None] * pos)):
        for k in range(3):
            part = v.astype(np.float16)
            v = v - part.astype(np.float64)
            qinit[:, 24 + 3 * n + k] = part.reshape(4, 4, SEQ)
    kinit[:, 24:27], kinit[:, 27:32] = pos, 1.0
    arrays["qinit"], arrays["kinit"] = qinit.reshape(P, 4, SEQ), kinit.reshape(P, 4, SEQ)
    future = np.triu(np.ones((P, P)), 1) * -4e9
    arrays["maskq"], arrays["maskk"] = np.tile(future, (1, 4)).astype(bf), np.tile(future.T, (1, 4)).astype(bf)
    arrays["identh"] = np.eye(P, dtype=np.float16)
    arrays["tri"] = np.triu(np.ones((P, P), np.float32))
    arrays["later"] = np.tril(np.ones((P, P), np.float32), -1)
    bf = ml_dtypes.bfloat16
    arrays["ident"] = np.eye(P, dtype=np.float32)
    arrays["identb"] = np.eye(P).astype(bf)
    arrays["experts"] = np.broadcast_to(np.arange(E0, dtype=np.float32), (P, GT, E0))
    for name, e, i in (("sel0", E0, I0), ("sel1", E1 + 1, I1)):
        s = np.tile(np.repeat(np.eye(e), i, axis=1), (3, 1))
        arrays[name] = cat(s, np.zeros((P - 3 * e, e * i))).astype(bf)

    nc = _bacc.Bacc("TRN2", target_bir_lowering=False, num_devices=1)
    io, feed = {}, {}
    for name, v in arrays.items():
        feed[name + "_dram"] = np.ascontiguousarray(v)
        io[name] = nc.dram_tensor(name + "_dram", v.shape, mybir.dt.from_np(v.dtype), kind="ExternalInput").ap()
    io["out"] = nc.dram_tensor("out_dram", a["L0_attn_u"].shape, F32, kind="ExternalOutput").ap()
    build(nc, io, _phases)
    r = _run(nc, [feed], core_ids=[0])
    return r.results[0]["out_dram"]
```

```python
from contextlib import ExitStack

import concourse.bass as bass
from concourse import mybir

ACT = mybir.ActivationFunctionType
ALU = mybir.AluOpType
F32 = mybir.dt.float32
F16 = mybir.dt.float16
BF16 = mybir.dt.bfloat16
U32 = mybir.dt.uint32
AX = mybir.AxisListType.X

P = 128
SEQ = 256
NSEQ = 16
TOK = NSEQ * SEQ
TILES = TOK // P
GROUP = 512
GT = GROUP // P
NG = TOK // GROUP
EPS = 1e-5
WSCALE = 16.0

E0, I0 = 16, 88
E1, I1 = 8, 256
NT0 = E0 * I0 // P
NT1 = (E1 + 1) * I1 // P
LAG = 3
HRING = 6
FRING = 3
POWERS_AT = 7
CHUNKS = {"F0": 1, "F1": GT}
TOP_AT = {"F0": 8, "F1": POWERS_AT + GT + 1}
GATES_AT = {"F0": 9, "F1": POWERS_AT + GT + 3}
GATES_T_AT = {"F0": NT0 - 1, "F1": POWERS_AT + GT + 5}

HEADS, HD, STATE, TAPS = 4, 64, 64, 4
INNER = HEADS * HD
CH = INNER + 2 * STATE
CS = 256.0
PAD = 4

MAMBA = dict(seg_ready=4, cum_ready=1, g_ready=2, dt_ready=1, yd_ready=2, yoff_ready=1, convx_ready=2, convb_ready=1,
             convc_ready=1, u2_ready=2, hnT_ready=2, y_ready=1,
             decay_ready=4, ed_ready=1, goff_ready=2, e_ready=1, sp_ready=1, bc_biased=2, gelu_ready=2, hnT0_copied=1,
             gm_ready=2, mt_ready=4, dtc_ready=1, d_ready=1, mixed=1, hvar_ready=1, hn_ready=1, xc_biased=2,
             xneg_ready=1, bcneg_ready=2, xs_val=1, bc_val=2, hnT1_copied=1,
             trid_ready=4, xs_ready=1, hrstd_ready=1, x_biased=1)

AH, AD = 16, 8
UNITS = [(0, 0), (1, 0), (1, 1)]
NU = 2 * len(UNITS)
REGROUP, SPREAD = 16 * 3, 16 * 4
MAXIMA = 16 * 2
PRING = 3
ROWS = 30
ATTN = dict(s1_ready=NU, max_ready=NU, s2_ready=NU, exp_ready=NU, plo_ready=NU, pv_done=NU, qk_ready=1, rope_mul=1, roped=1,
            part_hi=1, part_lo=1, v_ready=1, v_copied=1, vlo_ready=1, negmax=1, mT_ready=1, mrow_ready=1, onorm=1, oTa_ready=1,
            oTa_copied=1, ya_ready=1)

PER_TILE = ("a_ready", "u_ready", "gx_ready", "silu_ready", "m_ready", "h_ready", "hhi_ready", "hlo_ready", "h_used")
PER_GROUP = ("var_ready", "rstd_ready", "xn_ready", "xnT_ready", "xhi_ready", "xlo_ready", "logits_ready",
             "power_in", "power_out", "gates_ready", "gatesT_ready", "gT_ready", "o_copied",
             "outT_ready", "x_updated")


def build(nc, io, phases):
    ctx = ExitStack()
    with ctx:
        def sb(name, shape, dt=F32):
            return ctx.enter_context(nc.sbuf_tensor(name, shape, dt))

        def bank(name):
            return ctx.enter_context(nc.psum_tensor(name, [P, 512], F32))

        def sem(name):
            return ctx.enter_context(nc.semaphore(name))

        S = {n: sem(n) for n in PER_TILE + PER_GROUP + tuple(MAMBA) + tuple(ATTN)}
        x_loaded = [sem(f"x_loaded{g}") for g in range(NG)]
        consts_loaded, idents_loaded = sem("consts_loaded"), sem("idents_loaded")
        w_loaded = {n: sem(f"{n}_loaded") for n in ("w1g0", "w1u0", "w20", "w1g1", "w1u1", "w21")}
        mamba_loaded, wc_ready, wchi_ready = sem("mamba_loaded"), sem("wc_ready"), sem("wchi_ready")
        attn_loaded, maxima_done = sem("attn_loaded"), sem("maxima_done")
        spread_done = [sem(f"spread_done{k}") for k in range(2)]
        regrouped = sem("regrouped")
        regroup = nc.dram_tensor("regroup", (2, 2, 32, 4, 4, SEQ), F16).ap()
        aprep_act, aprep_dve = sem("aprep_act"), sem("aprep_dve")
        mprep_act, mprep_dve = sem("mprep_act"), sem("mprep_dve")
        whi_ready, wlo_ready, out_stored = sem("whi_ready"), sem("wlo_ready"), sem("out_stored")
        dve_step, pool_step = sem("dve_step"), sem("pool_step")

        class Arena:
            def __init__(self, name, words):
                self.mem, self.words, self.at = sb(name, [P, words]), words, 0

            def restart(self):
                self.at = 0

            def take(self, shape, dt=F32):
                n = 1
                for d in shape[1:]:
                    n *= d
                words = n * (1 if dt == F32 else 2) // (1 if dt == F32 else 4)
                v = self.mem[0:shape[0], self.at:self.at + words]
                self.at += words
                assert self.at <= self.words
                if dt != F32:
                    v = v.bitcast(dt)
                names = "abcd"[:len(shape) - 1]
                return v.rearrange(f"p ({' '.join(names)}) -> p {' '.join(names)}", **dict(zip(names, shape[1:])))

        tiles_mem, tokens_mem = Arena("tiles_mem", 7168), Arena("tokens_mem", TOK)
        stage_mem, conv_mem = Arena("stage_mem", NT1 * P), Arena("conv_mem", CH // P * TAPS * CH)
        x = sb("x", [P, TILES, P])
        xn = sb("xn", [P, GT, P])
        xhi, xlo = tokens_mem.take([P, TOK], F16), tokens_mem.take([P, TOK], F16)
        stats, mv = sb("stats", [P, GT, 6]), sb("mv", [P, GT, 2])
        vpe, rstd = sb("vpe", [P, GT]), sb("rstd", [P, GT])
        neghalf, eps, euler = sb("neghalf", [P, GT]), sb("eps", [P, GT]), sb("euler", [P, GT, E1])
        ident, identb = sb("ident", [P, P]), sb("identb", [P, P], BF16)
        experts = sb("experts", [P, GT, E0])
        stage0, stage = tiles_mem.take([P, 3, NT0 * P]), stage_mem.take([P, NT1 * P])
        tiles_mem.restart()
        W = {}
        for k, nt in ((0, NT0), (1, NT1)):
            for n in ("w1g", "w1u", "w2"):
                W[n, k] = (sb(f"{n}{k}hi", [P, nt * P], F16), sb(f"{n}{k}lo", [P, nt * P], F16))
        sel = {0: sb("sel0", [P, NT0 * P], BF16), 1: sb("sel1", [P, NT1 * P], BF16)}
        wr = {0: sb("wr0", [P, E0]), 1: sb("wr1", [P, E1])}
        wrs = {0: sb("wrs0", [P, 2, E0], F16), 1: sb("wrs1", [P, 2, E1], F16)}
        rb = sb("rb", [P, E1])
        lg = sb("lg", [P, GT, E0])
        top = sb("top", [P, GT, 8])
        topi = sb("topi", [P, GT, 8], U32)
        topf = sb("topf", [P, GT, 2])
        pin, pout = sb("pin", [P, GT, E1]), sb("pout", [P, GT, E1])
        gw = sb("gw", [P, GT, 2])
        eq = sb("eq", [P, 2, GT, E0])
        gate = sb("gate", [P, GT, E0])
        gres = sb("gres", [P, GT, E0])
        gparts = sb("gparts", [P, GT, P], BF16)
        gT = sb("gT", [P, TOK], BF16)
        silu = tiles_mem.take([P, 2, 512])
        m = tiles_mem.take([P, 2, 512])
        h = tiles_mem.take([P, FRING, 512])
        hhi, hlo = tiles_mem.take([P, HRING, 512], F16), tiles_mem.take([P, HRING, 512], F16)
        oT = tiles_mem.take([P, 512])

        tri, later = sb("tri", [P, P]), sb("later", [P, P])
        win1 = sb("win1", [P, CH // P, P])
        convw = conv_mem.take([P, CH // P, TAPS, CH])
        wc = [sb("wchi", [P, TAPS, CH], F16), sb("wclo", [P, TAPS, CH], F16)]
        wdt, win2, w3 = sb("wdt", [P, HEADS]), sb("win2", [P, INNER]), sb("w3", [P, 2, P])
        wdts, win2s = sb("wdts", [P, 2, HEADS], F16), sb("win2s", [P, 2, INNER], F16)
        lng, lnb = sb("lng", [P, 2]), sb("lnb", [P, 2])
        lnbw, w3g, b3 = sb("lnbw", [P, 2, P]), sb("w3g", [P, 2, P]), sb("b3", [P, P])
        xbias, bcbias, slope = sb("xbias", [P, INNER]), sb("bcbias", [STATE, 2]), sb("slope", [P, 1])
        alog, rate = sb("alog", [P, HEADS]), sb("rate", [P, HEADS])
        xm = [sb("xmhi", [P, 2, PAD + SEQ], F16), sb("xmlo", [P, 2, PAD + SEQ], F16)]
        dt, dtc, dtx, de, sp, dd = (sb(n, [P, GT, HEADS]) for n in ("dt", "dtc", "dtx", "de", "sp", "dd"))
        for arena in (tiles_mem, tokens_mem, stage_mem, conv_mem):
            arena.restart()
        trid, decay, mt = (tiles_mem.take([P, GT, HEADS * P]) for _ in range(3))
        ed = sb("ed", [P, 2, 2, HEADS])
        gm, goff = sb("gm", [P, GT, P]), sb("goff", [P, 2, P])
        xc, xneg, xv, hm = (tokens_mem.take([P, GT, INNER]) for _ in range(4))
        bcc, bcneg, bcv = (conv_mem.take([STATE, 2, GROUP]) for _ in range(3))
        xsd = conv_mem.take([P, 2, INNER])
        u2 = tiles_mem.take([P, GT, INNER])
        yo = conv_mem.take([P, 2, INNER])
        hn = stage_mem.take([P, GT, INNER])
        hnT = stage_mem.take([P, 2, GROUP])
        hstats, hmv, hvpe, hrstd = sb("hstats", [P, GT, 6]), sb("hmv", [P, GT, 2]), sb("hvpe", [P, GT]), sb("hrstd", [P, GT])

        qka = [sb(f"qka{k}", [P, 2, 4, SEQ], F16) for k in range(2)]
        qa, ka = ([t[:, n, :, :] for t in qka] for n in range(2))
        xa = [sb("xahi", [P, GROUP], F16), sb("xalo", [P, GROUP], F16)]
        ropec, ropes = sb("ropec", [P, SEQ]), sb("ropes", [P, SEQ])
        maskq, maskk = sb("maskq", [P, P], BF16), sb("maskk", [P, 512], BF16)
        identh = sb("identh", [P, P], F16)
        wqk, wv = sb("wqk", [P, 4 * P]), sb("wv", [P, P])
        wqks, wvs = sb("wqks", [P, 2, 4 * P], F16), sb("wvs", [P, 2, P], F16)
        wo, obias = sb("wo", [P, P]), sb("obias", [P, P])
        tiles_mem.restart(), tokens_mem.restart(), stage_mem.restart()
        masked = stage_mem.take([P, 2, 8, P])
        pt = tiles_mem.take([P, 2, 1024])
        phi, plo = tiles_mem.take([P, PRING, 1024], F16), tiles_mem.take([P, PRING, 1024], F16)
        rope = tiles_mem.take([P, 2, 2, SEQ])
        qk = tiles_mem.take([P, 2, SEQ])
        qks = tiles_mem.take([P, 2, 2, SEQ], F16)
        va = tokens_mem.take([P, 2, 2, 2, AH * (AD + 1)], F16)
        mx = tokens_mem.take([P, 3, AH])
        negm = tokens_mem.take([P, 2, AH])
        mparts = tokens_mem.take([P, 2, 2 * AH], F16)
        mrow = tokens_mem.take([2 * 4, 4, SEQ], F16)
        orec = tokens_mem.take([P, 2, AH])
        on = tokens_mem.take([P, 2, P])
        oTa = tokens_mem.take([P, SEQ])

        sets = [ctx.enter_context(nc.psum_tensor(f"set{k}", [P, 1024], F32)) for k in range(3)]
        bA, bU, bG = ([s[:, 0:512], s[:, 512:1024]] for s in sets)
        bO, bT = bank("bO"), bank("bT")
        mTh = sets[1][:, 512:1024].bitcast(F16)
        mX, mB, mC, mU, mY = [bA[0], bO], bU[0], bU[1], bG, bA[1]
        mSeg, mG, mCum = [bG[0], bG[1], bU[0], bU[1]], [bO, bA[0]], bA[1]
        bTb = bT[:, :].bitcast(BF16)

        NT = {"F0": NT0, "F1": NT1}
        SHARED = ("var_ready", "rstd_ready", "xn_ready", "xnT_ready", "xhi_ready", "xlo_ready", "x_updated")
        BY_SEQ = ("xnT_ready", "xhi_ready", "xlo_ready", "x_updated")
        base = []
        tally = {n: 0 for n in S}
        for ph in phases:
            base.append(dict(tally))
            if ph in NT:
                for n in PER_TILE:
                    tally[n] += NG * NT[ph]
                for n in PER_GROUP:
                    tally[n] += NG
            else:
                for n in SHARED:
                    tally[n] += NG
                if ph == "M":
                    for n, k in MAMBA.items():
                        tally[n] += NG * k
                else:
                    for n, k in ATTN.items():
                        tally[n] += NSEQ * k
                    for n in BY_SEQ:
                        tally[n] += NSEQ - NG
                    tally["x_biased"] += NG

        def wait(eng, name, value):
            if not isinstance(value, int) or value > 0:
                eng.wait_ge(S[name], value)

        def wait_apart(eng, name, value):
            if not isinstance(value, int):
                eng.wait_ge(consts_loaded, ALL_CONSTS)
            wait(eng, name, value)

        class Chain:
            def __init__(self, eng, s):
                self.eng, self.s, self.at, self.k = eng, s, 0, 0

            def add(self, ins):
                ins.then_inc(self.s, 1)
                self.k += 1

            def join(self):
                self.eng.drain()

            def link(self, ins):
                self.add(ins)
                self.join()

        def groups(eng, emit, chain=None, per=0):
            emit(0)
            if chain:
                start = chain.at + chain.k
                chain.k = 0
            with eng.Fori(1, NG - 1) as g:
                if chain:
                    chain.at = start + (g - 1) * per
                emit(g)
                if chain:
                    assert chain.k == per, chain.k
            if chain:
                chain.at, chain.k = start + (NG - 2) * per, 0
            emit(NG - 1)

        class Seq:
            def __init__(self, value, index=None, half=None):
                self.value = value
                self.half = value // 2 if half is None else half
                self.index = value if index is None else index
                self.parity = self.index % 2

            def plus(self, n):
                return Seq(self.value + n, self.index + n, self.half + (self.parity + n) // 2)

        def steps(eng, step):
            for q in (0, 1):
                step(Seq(q))
            with eng.Fori(1, NG - 2) as g:
                for s in range(2):
                    step(Seq(2 * g + s, 4 + s, g))
            for q in range(NSEQ - 4, NSEQ):
                step(Seq(q))

        def is_first(g):
            return isinstance(g, int) and g == 0

        def is_last(g):
            return isinstance(g, int) and g == NG - 1

        MLOADS = [("tri", tri), ("later", later), ("win1", win1), ("convw", convw), ("wdt", wdt), ("win2", win2), ("w3", w3),
                  ("lng", lng), ("lnb", lnb), ("xbias", xbias), ("bcbias", bcbias), ("slope", slope), ("alog", alog)]
        ALOADS = [("ropec", ropec), ("ropes", ropes),
                  ("maskq", maskq), ("maskk", maskk), ("identh", identh), ("wqk", wqk), ("wv", wv), ("wo", wo), ("obias", obias)]
        ALL_ALOADS = 16 * (len(ALOADS) + 4)
        ALL_MLOADS = 16 * len(MLOADS)

        def pair(buf):
            return buf[:, :, PAD:]

        block = ctx.enter_context(nc.Block())
        x_dram = io["x"].rearrange("b (h p) d -> p (b h) d", p=P)
        y_dram = io["out"].rearrange("b (h p) d -> p (b h) d", p=P)

        NAMES = ("w1g", "w1u", "w2")
        EARLY, ALL_WEIGHTS = len(NAMES) + 2, 2 * len(NAMES) + 2
        CONSTS = [("experts", experts[:, :, :]), ("sel0", sel[0][:, :]), ("sel1", sel[1][:, :]),
                  ("wr0", wr[0][:, :]), ("wr1", wr[1][:, :]), ("rb", rb[:, :])]
        ALL_CONSTS = 16 * len(CONSTS)
        W_AT = (1, 5, 9)

        @block.sync
        def _(sp):
            for n, dst in (("ident", ident), ("identb", identb)):
                sp.dma_start(dst[:, :], io[n]).then_inc(idents_loaded, 16)
            sp.dma_start(x[:, 0:GT, :], x_dram[:, 0:GT, :]).then_inc(x_loaded[0], 16)
            for n, name in enumerate(NAMES):
                sp.dma_start(stage0[:, n, :], io[f"{name}0"]).then_inc(w_loaded[f"{name}0"], 16)
            for g in range(1, NG):
                sp.dma_start(x[:, g * GT:(g + 1) * GT, :], x_dram[:, g * GT:(g + 1) * GT, :]).then_inc(x_loaded[g], 16)
            sp.dma_start(stage[:, :], io[f"{NAMES[0]}1"]).then_inc(w_loaded[f"{NAMES[0]}1"], 16)
            for n, dst in MLOADS:
                src = io[n].partition_broadcast(P) if n in ("xbias", "slope", "alog") else io[n]
                sp.dma_start(dst[tuple([slice(None)] * len(dst.shape))], src).then_inc(mamba_loaded, 16)
            for n, dst in ALOADS:
                src = io[n].partition_broadcast(P) if n == "obias" else io[n]
                sp.dma_start(dst[tuple([slice(None)] * len(dst.shape))], src).then_inc(attn_loaded, 16)

            for a in range(2):
                for n, name in enumerate(("qinit", "kinit")):
                    src = io[name].rearrange("(i r) j s -> r i j s", i=4)
                    sp.dma_start(regroup[a, n, 3 * AD:], src[3 * AD:]).then_inc(attn_loaded, 16)

            for n, name in enumerate(NAMES[1:]):
                sp.wait_ge(wlo_ready, EARLY + n + 1)
                sp.dma_start(stage[:, :], io[f"{name}1"]).then_inc(w_loaded[f"{name}1"], 16)

            def attention(b):
                def write_parts(q):
                    if q.index >= 2:
                        sp.wait_ge(consts_loaded, ALL_CONSTS)
                        sp.wait_ge(spread_done[q.parity], SPREAD * q.half)
                    wait_apart(sp, "part_lo", b["part_lo"] + q.value + 1)
                    parts = qks[:, :, :, :].rearrange("p n a s -> p (n a) s")
                    for c, pick in enumerate((slice(0, 3, 2), slice(1, 3), slice(0, 4, 3))):
                        dst = regroup[q.parity, :, AD * c:AD * (c + 1)].rearrange("n e i j s -> (e i j) n s")
                        sp.dma_start(dst, parts[:, pick, :]).then_inc(regrouped, 16)

                def spread(q):
                    sp.wait_ge(consts_loaded, ALL_CONSTS)
                    sp.wait_ge(regrouped, REGROUP * (q.value + 1))
                    if q.index >= 2:
                        wait(sp, "s2_ready", NU * q.value + (b["s2_ready"] - NU))
                    for i in range(4):
                        sp.dma_start(qka[q.parity][32 * i:32 * (i + 1), :, :, :], regroup[q.parity, :, :, i].rearrange("n r j s -> r n j s"))\
                          .then_inc(spread_done[q.parity], 16)

                def maxima(q):
                    wait_apart(sp, "mrow_ready", b["mrow_ready"] + q.value + 1)
                    for c in range(2):
                        sp.dma_start(qa[q.parity][ROWS + c::32, :, :], mrow[4 * c:4 * c + 4, :, :]).then_inc(maxima_done, 16)

                def step(q):
                    if q.index < NSEQ - 2:
                        write_parts(q.plus(2))
                        spread(q.plus(2))
                    if q.index < NSEQ - 1:
                        maxima(q.plus(1))
                for q in (Seq(0), Seq(1)):
                    write_parts(q)
                    spread(q)
                maxima(Seq(0))
                steps(nc.sync, step)
            for ph, b in zip(phases, base):
                if ph == "A":
                    attention(b)
            sp.wait_ge(S["x_updated"], tally["x_updated"])
            sp.dma_start(y_dram, x[:, :, :]).then_inc(out_stored, 16)
            sp.wait_ge(out_stored, 16)

        @block.gpsimd
        def _(pool):
            ch = Chain(pool, pool_step)
            ch.add(pool.memset(gT[:, :].bitcast(U32), 0))
            ch.add(pool.memset(gparts[:, :, :].bitcast(U32), 0))
            ch.add(pool.memset(eps[:, :], EPS))
            ch.add(pool.memset(neghalf[:, :], -0.5))
            ch.add(pool.memset(euler[:, :, :], 2.718281828459045))
            for n, dst in CONSTS:
                src = io[n].partition_broadcast(P) if n == "rb" else io[n]
                pool.dma_start(dst, src).then_inc(consts_loaded, 16)
            ch.join()

            def rsqrt(b, g):
                wait(pool, "var_ready", b["var_ready"] + g + 1)
                ch.link(pool.tensor_tensor(vpe[:, :], mv[:, :, 1], eps[:, :], ALU.add))
                pool.tensor_tensor(rstd[:, :], vpe[:, :], neghalf[:, :], ALU.pow).then_inc(S["rstd_ready"], 1)

            def powers(b, g, kind, i):
                if i == 0:
                    wait(pool, "power_in", b["power_in"] + g + 1)
                if kind == "F0":
                    pool.tensor_tensor(pout[:, :, 0:1], euler[:, :, 0:1], pin[:, :, 0:1], ALU.pow).then_inc(S["power_out"], 1)
                else:
                    ins = pool.tensor_tensor(pout[:, i, :], euler[:, i, :], pin[:, i, :], ALU.pow)
                    if i < GT - 1:
                        ch.add(ins)
                    else:
                        ins.then_inc(S["power_out"], 1)

            def layer(kind, b):
                nt = NT[kind]

                def group(g):
                    for j in range(nt):
                        t = nt * g + j
                        wait(pool, "hhi_ready", b["hhi_ready"] + t + 1)
                        r, f = j % HRING, j % FRING
                        pool.tensor_tensor(hlo[:, r, :], h[:, f, :], hhi[:, r, :], ALU.subtract).then_inc(S["hlo_ready"], 1)
                        if not is_last(g):
                            if j == 0:
                                rsqrt(b, g + 1)
                            if 0 <= j - POWERS_AT < CHUNKS[kind]:
                                powers(b, g + 1, kind, j - POWERS_AT)
                rsqrt(b, 0)
                for i in range(CHUNKS[kind]):
                    powers(b, 0, kind, i)
                groups(nc.gpsimd, group, ch, CHUNKS[kind])

            def mamba(b):
                def x_bias(g):
                    wait(pool, "xn_ready", b["xn_ready"] + g + 1)
                    dst = x[:, bass.ts(g, GT), :]
                    pool.tensor_tensor(dst, dst, b3[:, :].unsqueeze(1).broadcast_to([P, GT, P]), ALU.add).then_inc(S["x_biased"], 1)

                def hidden_rsqrt(g):
                    wait(pool, "hvar_ready", b["hvar_ready"] + g + 1)
                    ch.link(pool.tensor_tensor(hvpe[:, :], hmv[:, :, 1], eps[:, :], ALU.add))
                    pool.tensor_tensor(hrstd[:, :], hvpe[:, :], neghalf[:, :], ALU.pow).then_inc(S["hrstd_ready"], 1)

                def scaled_x(g):
                    wait(pool, "ed_ready", b["ed_ready"] + g + 1)
                    wait(pool, "xs_val", b["xs_val"] + g + 1)
                    wait(pool, "yoff_ready", b["yoff_ready"] + g)
                    for q in range(2):
                        ins = pool.tensor_tensor(xsd[:, q, :].rearrange("p (h d) -> p h d", d=HD),
                                                 xv[:, 2 * q, :].rearrange("p (h d) -> p h d", d=HD),
                                                 ed[:, 0, q, :].unsqueeze(2).broadcast_to([P, HEADS, HD]), ALU.mult)
                    ins.then_inc(S["xs_ready"], 1)

                def triangles(g):
                    wait(pool, "d_ready", b["d_ready"] + g + 1)
                    for t in range(GT):
                        wait(pool, "seg_ready", b["seg_ready"] + GT * g - GT + t + 1 if not is_first(g) else b["seg_ready"])
                        pool.tensor_tensor(trid[:, t, :].rearrange("p (h l) -> p h l", l=P),
                                           tri[:, :].unsqueeze(1).broadcast_to([P, HEADS, P]),
                                           dd[:, t, :].unsqueeze(2).broadcast_to([P, HEADS, P]), ALU.mult).then_inc(S["trid_ready"], 1)

                def body(g):
                    nxt = not is_last(g)
                    if nxt:
                        rsqrt(b, g + 1)
                    scaled_x(g)
                    if nxt:
                        x_bias(g + 1)
                    hidden_rsqrt(g)
                    if nxt:
                        triangles(g + 1)
                pool.wait_ge(mamba_loaded, ALL_MLOADS)
                pool.wait_ge(mprep_act, 3)
                rsqrt(b, 0)
                x_bias(0)
                triangles(0)
                with nc.gpsimd.Fori(0, NG - 1) as g:
                    body(g)
                body(NG - 1)

            def attention(b):
                def x_bias(g):
                    wait(pool, "xn_ready", b["xn_ready"] + g + 1)
                    dst = x[:, bass.ts(g, GT), :]
                    pool.tensor_tensor(dst, dst, obias[:, :].unsqueeze(1).broadcast_to([P, GT, P]), ALU.add).then_inc(S["x_biased"], 1)

                def rope_sum(q):
                    wait(pool, "rope_mul", b["rope_mul"] + q.value + 1)
                    wait(pool, "part_lo", b["part_lo"] + q.value)
                    pool.tensor_tensor(qk[:, :, :], rope[:, :, 0, :], rope[:, :, 1, :], ALU.add).then_inc(S["roped"], 1)

                def part_lo(q):
                    wait(pool, "part_hi", b["part_hi"] + q.value + 1)
                    pool.tensor_tensor(qks[:, :, 1, :], qk[:, :, :], qks[:, :, 0, :], ALU.subtract).then_inc(S["part_lo"], 1)

                def p_lo(q, u):
                    wait(pool, "exp_ready", b["exp_ready"] + NU * q.value + u + 1)
                    pool.tensor_tensor(plo[:, u % PRING, :], pt[:, u % 2, :], phi[:, u % PRING, :], ALU.subtract).then_inc(S["plo_ready"], 1)

                def step(q):
                    normed = q.index < NSEQ - 3 and q.parity == 1
                    if normed:
                        rsqrt(b, q.half + 2)
                    if q.index < NSEQ - 2:
                        rope_sum(q.plus(2))
                    for u in range(NU):
                        p_lo(q, u)
                        if u == 1 and q.index < NSEQ - 2:
                            part_lo(q.plus(2))
                        if u == 2 and normed:
                            x_bias(q.half + 2)
                pool.wait_ge(attn_loaded, ALL_ALOADS)
                rsqrt(b, 0)
                x_bias(0)
                for q in (Seq(0), Seq(1)):
                    rope_sum(q)
                    part_lo(q)
                rsqrt(b, 1)
                x_bias(1)
                steps(nc.gpsimd, step)
            for ph, b in zip(phases, base):
                {"M": mamba, "A": attention}[ph](b) if ph in "MA" else layer(ph, b)

        def last_user(nt, j, n):
            if j >= n:
                return j - n
            return max(i for i in range(nt) if i % n == j % n) - nt

        def wait_slot(eng, name, b, nt, g, j, n):
            prev = last_user(nt, j, n)
            if is_first(g) and prev < 0:
                wait(eng, name, b[name])
            else:
                wait(eng, name, b[name] + nt * g + prev + 1)

        @block.scalar
        def _(act):
            for n, name in enumerate(NAMES):
                act.wait_ge(w_loaded[f"{name}0"], 16)
                act.activation(W[name, 0][0][:, :], stage0[:, n, :], ACT.Copy, scale=WSCALE).then_inc(whi_ready, 1)
            act.wait_ge(consts_loaded, ALL_CONSTS)
            for k in (0, 1):
                act.activation(wrs[k][:, 0, :], wr[k][:, :], ACT.Copy, scale=WSCALE).then_inc(whi_ready, 1)

            def w_hi(n):
                act.wait_ge(w_loaded[f"{NAMES[n]}1"], 16)
                act.activation(W[NAMES[n], 1][0][:, :], stage[:, :], ACT.Copy, scale=WSCALE).then_inc(whi_ready, 1)

            def x_hi(b, g):
                wait(act, "xnT_ready", b["xnT_ready"] + g + 1)
                act.activation(xhi[:, bass.ts(g, GROUP)], bT[:, :], ACT.Copy).then_inc(S["xhi_ready"], 1)

            def gates_out(b, g, kg):
                wait(act, "gatesT_ready", b["gatesT_ready"] + g + 1)
                act.activation(gT[0:kg, bass.ts(g, GROUP)], bTb[0:kg, 0:GROUP], ACT.Copy).then_inc(S["gT_ready"], 1)

            def out_copy(b, g, nt):
                wait(act, "h_used", b["h_used"] + nt * (g + 1))
                wait(act, "outT_ready", b["outT_ready"] + g)
                act.activation(oT[:, :], bO[:, :], ACT.Copy, scale=0.5 / WSCALE ** 2).then_inc(S["o_copied"], 1)

            def layer(kind, b):
                nt, kg = NT[kind], 3 * (E0 if kind == "F0" else E1 + 1)

                def h_hi(g, j, t):
                    wait(act, "h_ready", b["h_ready"] + t + 1)
                    wait_slot(act, "h_used", b, nt, g if j >= 0 else g - 1, j % nt, HRING)
                    act.activation(hhi[:, j % nt % HRING, :], h[:, j % nt % FRING, :], ACT.Copy).then_inc(S["hhi_ready"], 1)

                def group(g):
                    for j in range(nt):
                        t = nt * g + j
                        wait(act, "a_ready", b["a_ready"] + t + 1)
                        wait_slot(act, "m_ready", b, nt, g, j, 2)
                        act.activation(silu[:, j % 2, :], bA[j % 2][:, :], ACT.Silu, scale=1.0 / WSCALE).then_inc(S["silu_ready"], 1)
                        if j > 0:
                            h_hi(g, j - 1, t - 1)
                        if j == 2 and not is_first(g):
                            out_copy(b, g - 1, nt)
                        if b is base[0] and kind == "F0" and is_first(g) and j in W_AT:
                            w_hi(W_AT.index(j))
                        if not is_last(g):
                            if j == 5:
                                x_hi(b, g + 1)
                            if j == min(GATES_T_AT[kind] + 1, nt - 1):
                                gates_out(b, g + 1, kg)
                    h_hi(g, nt - 1, nt * g + nt - 1)
                x_hi(b, 0)
                gates_out(b, 0, kg)
                groups(nc.scalar, group)
                out_copy(b, NG - 1, nt)

            def mamba(b):
                def prepare():
                    act.wait_ge(mamba_loaded, ALL_MLOADS)
                    act.activation(rate[:, :], alog[:, :], ACT.Exp).then_inc(mprep_act, 1)
                    act.wait_ge(wc_ready, TAPS + 1)
                    act.activation(b3[:, :], bT[:, 0:P], ACT.Copy).then_inc(mprep_act, 1)
                    for k in range(TAPS):
                        act.activation(wc[0][:, k, :], [bA[0], bA[1], bU[0], bU[1]][k][:, 0:CH], ACT.Copy, scale=CS).then_inc(wchi_ready, 1)
                    act.activation(wdts[:, 0, :], wdt[:, :], ACT.Copy, scale=CS).then_inc(wchi_ready, 1)
                    act.activation(win2s[:, 0, :], win2[:, :], ACT.Copy, scale=CS).then_inc(mprep_act, 1)

                def decays(g):
                    for t in range(GT):
                        wait(act, "seg_ready", b["seg_ready"] + GT * g + t + 1)
                        wait(act, "mt_ready", b["mt_ready"] + GT * g)
                        act.activation(decay[:, t, :], mSeg[t][:, :], ACT.Exp, scale=-1.0).then_inc(S["decay_ready"], 1)
                    wait(act, "cum_ready", b["cum_ready"] + g + 1)
                    wait(act, "mixed", b["mixed"] + g)
                    act.activation(ed[:, :, :, :], mCum[:, 0:4 * HEADS].rearrange("p (a q h) -> p a q h", a=2, q=2),
                                   ACT.Exp, scale=-1.0).then_inc(S["ed_ready"], 1)

                def g_off(g):
                    for q in range(2):
                        wait(act, "gm_ready", b["gm_ready"] + 2 * g + q + 1)
                        wait(act, "yoff_ready", b["yoff_ready"] + g)
                        act.activation(goff[:, q, :], mG[q][:, P:2 * P], ACT.Copy).then_inc(S["goff_ready"], 1)

                def x_hi_pair(g):
                    wait(act, "xnT_ready", b["xnT_ready"] + g + 1)
                    wait(act, "u2_ready", b["u2_ready"] + 2 * g)
                    act.activation(pair(xm[0]), bT[:, :].rearrange("p (q s) -> p q s", q=2), ACT.Copy).then_inc(S["xhi_ready"], 1)

                def softplus(g):
                    wait(act, "dtc_ready", b["dtc_ready"] + g + 1)
                    act.activation(de[:, :, :], dtc[:, :, :], ACT.Exp).then_inc(S["e_ready"], 1)
                    wait(act, "e_ready", b["e_ready"] + g + 1)
                    act.activation(sp[:, :, :], de[:, :, :], ACT.Ln, bias=1.0).then_inc(S["sp_ready"], 1)

                def bc_bias(g):
                    for n, (s, bk) in enumerate((("convb_ready", mB), ("convc_ready", mC))):
                        wait(act, s, b[s] + g + 1)
                        wait(act, "bc_val", b["bc_val"] + 2 * g)
                        act.activation(bcc[:, n, :], bk[0:STATE, :], ACT.Identity, scale=1.0 / CS, bias=bcbias[:, n:n + 1]).then_inc(S["bc_biased"], 1)

                def gelu(g):
                    for n in range(2):
                        wait(act, "u2_ready", b["u2_ready"] + 2 * g + n + 1)
                        wait(act, "mixed", b["mixed"] + g)
                        act.activation(u2[:, 2 * n:2 * n + 2, :], mU[n][:, :].rearrange("p (t c) -> p t c", t=2), ACT.Gelu, scale=1.0 / CS)\
                           .then_inc(S["gelu_ready"], 1)

                def hnT_copy(g):
                    wait(act, "hnT_ready", b["hnT_ready"] + 2 * g + 1)
                    wait(act, "y_ready", b["y_ready"] + g)
                    act.activation(hnT[:, 0, :], mY[:, :], ACT.Copy).then_inc(S["hnT0_copied"], 1)

                def body(g):
                    nxt = not is_last(g)
                    decays(g)
                    g_off(g)
                    if nxt:
                        x_hi_pair(g + 1)
                        softplus(g + 1)
                        bc_bias(g + 1)
                        gelu(g + 1)
                    hnT_copy(g)
                prepare()
                x_hi_pair(0)
                softplus(0)
                bc_bias(0)
                gelu(0)
                with nc.scalar.Fori(0, NG - 1) as g:
                    body(g)
                body(NG - 1)

            def attention(b):
                def prepare():
                    act.wait_ge(attn_loaded, ALL_ALOADS)
                    act.activation(wqks[:, 0, :], wqk[:, :], ACT.Copy, scale=WSCALE).then_inc(aprep_act, 1)
                    act.activation(wvs[:, 0, :], wv[:, :], ACT.Copy, scale=WSCALE).then_inc(aprep_act, 1)

                def x_hi(q):
                    wait(act, "xnT_ready", b["xnT_ready"] + q.value + 1)
                    if q.index >= 2:
                        wait(act, "v_ready", b["v_ready"] + q.value - 1)
                    act.activation(xa[0][:, q.parity * SEQ:(q.parity + 1) * SEQ], bT[:, 0:SEQ], ACT.Copy).then_inc(S["xhi_ready"], 1)

                def part_hi(q):
                    wait(act, "roped", b["roped"] + q.value + 1)
                    if q.index >= 1:
                        act.wait_ge(regrouped, REGROUP * q.value)
                    act.activation(qks[:, :, 0, :], qk[:, :, :], ACT.Copy).then_inc(S["part_hi"], 1)

                def v_copy(q):
                    wait(act, "v_ready", b["v_ready"] + q.value + 1)
                    if q.index >= 2:
                        wait(act, "pv_done", b["pv_done"] + NU * (q.value - 1))
                    for t in range(2):
                        dst = va[:, q.parity, t, 0, :].rearrange("p (h e) -> p h e", e=AD + 1)[:, :, 0:AD]
                        ins = act.activation(dst, sets[1][:, t * P:(t + 1) * P].rearrange("p (h e) -> p h e", e=AD), ACT.Copy, scale=1.0 / WSCALE)
                    ins.then_inc(S["v_copied"], 1)

                def exps(q, u):
                    wait(act, "s2_ready", b["s2_ready"] + NU * q.value + u + 1)
                    if q.index or u >= 2:
                        wait(act, "plo_ready", b["plo_ready"] + NU * q.value + u - 1)
                    if q.index or u >= PRING:
                        wait(act, "pv_done", b["pv_done"] + NU * q.value + u - PRING + 1)
                    src = sets[(2 * u + 1) % 3][:, :]
                    act.activation(pt[:, u % 2, :], src, ACT.Exp, scale=AD ** -0.5)
                    act.activation(phi[:, u % PRING, :], src, ACT.Exp, scale=AD ** -0.5).then_inc(S["exp_ready"], 1)

                def m_copy(q):
                    wait(act, "mT_ready", b["mT_ready"] + q.value + 1)
                    if q.index >= 1:
                        act.wait_ge(maxima_done, MAXIMA * q.value)
                    act.activation(mrow[:, :, :], mTh[0:8, :].rearrange("p (j s) -> p j s", j=4), ACT.Copy).then_inc(S["mrow_ready"], 1)

                def o_copy(q):
                    wait(act, "oTa_ready", b["oTa_ready"] + q.value + 1)
                    wait(act, "ya_ready", b["ya_ready"] + q.value)
                    act.activation(oTa[:, :], bT[:, 0:SEQ], ACT.Copy).then_inc(S["oTa_copied"], 1)

                def step(q):
                    if q.index:
                        o_copy(q.plus(-1))
                    for u in range(NU):
                        exps(q, u)
                        if u == 1 and q.index < NSEQ - 2:
                            part_hi(q.plus(2))
                        if u == 4 and q.index < NSEQ - 3:
                            x_hi(q.plus(3))
                    if q.index < NSEQ - 1:
                        m_copy(q.plus(1))
                    if q.index < NSEQ - 2:
                        v_copy(q.plus(2))
                prepare()
                for q in (Seq(0), Seq(1)):
                    x_hi(q)
                    part_hi(q)
                for q in (Seq(0), Seq(1)):
                    v_copy(q)
                x_hi(Seq(2))
                m_copy(Seq(0))
                steps(nc.scalar, step)
                o_copy(Seq(NSEQ - 1))
            for ph, b in zip(phases, base):
                {"M": mamba, "A": attention}[ph](b) if ph in "MA" else layer(ph, b)

        @block.vector
        def _(dve):
            ch = Chain(dve, dve_step)
            for n, name in enumerate(NAMES):
                dve.wait_ge(whi_ready, n + 1)
                dve.scalar_tensor_tensor(W[name, 0][1][:, :], stage0[:, n, :], WSCALE, W[name, 0][0][:, :],
                                         ALU.mult, ALU.subtract).then_inc(wlo_ready, 1)
            dve.wait_ge(whi_ready, EARLY)
            for k in (0, 1):
                dve.scalar_tensor_tensor(wrs[k][:, 1, :], wr[k][:, :], WSCALE, wrs[k][:, 0, :],
                                         ALU.mult, ALU.subtract).then_inc(wlo_ready, 1)

            def w_lo(n):
                dve.wait_ge(whi_ready, EARLY + n + 1)
                dve.scalar_tensor_tensor(W[NAMES[n], 1][1][:, :], stage[:, :], WSCALE, W[NAMES[n], 1][0][:, :],
                                         ALU.mult, ALU.subtract).then_inc(wlo_ready, 1)

            def xs(g, i):
                return x[:, bass.ds(GT * g + i, 1), :].squeeze(1) if not isinstance(g, int) else x[:, GT * g + i, :]

            def ln_stats(b, g):
                for i in range(GT):
                    ch.add(dve.bn_stats(stats[:, i, :], xs(g, i)))
                ch.join()
                for i in range(GT):
                    ins = dve.bn_aggr(mv[:, i, :], stats[:, i, :])
                    if i < GT - 1:
                        ch.add(ins)
                    else:
                        ins.then_inc(S["var_ready"], 1)

            def ln_apply(b, g, per=1):
                wait_apart(dve, "var_ready", b["var_ready"] + g + 1)
                wait(dve, "rstd_ready", b["rstd_ready"] + g + 1)
                wait(dve, "xnT_ready", b["xnT_ready"] + per * g)
                for i in range(GT):
                    ins = dve.tensor_scalar(xn[:, i, :], xs(g, i), mv[:, i, 0:1], rstd[:, i:i + 1], ALU.subtract, ALU.mult)
                    if i < GT - 1:
                        ch.add(ins)
                    else:
                        ins.then_inc(S["xn_ready"], 1)

            def x_lo(b, g):
                wait(dve, "xhi_ready", b["xhi_ready"] + g + 1)
                dve.tensor_tensor(xlo[:, bass.ts(g, GROUP)], bT[:, :], xhi[:, bass.ts(g, GROUP)],
                                  ALU.subtract).then_inc(S["xlo_ready"], 1)

            def find_top(src, n):
                for i in range(GT):
                    ch.add(dve.max(top[:, i, :], src[:, i, 0:n]))
                ch.join()
                for i in range(GT):
                    ch.add(dve.max_index(topi[:, i, :], top[:, i, :], src[:, i, 0:n]))
                ch.join()
                ch.link(dve.tensor_copy(topf[:, :, :], topi[:, :, 0:2]))

            def route_begin(b, g, kind):
                wait(dve, "logits_ready", b["logits_ready"] + g + 1)
                wait(dve, "power_out", b["power_out"] + g)
                if kind == "F0":
                    ps = bT[:, 0:GT * E0].rearrange("p (t e) -> p t e", e=E0)
                    ch.link(dve.tensor_scalar(lg[:, :, :], ps, 1.0 / WSCALE, None, ALU.mult))
                    find_top(lg, E0)
                    dve.tensor_tensor(pin[:, :, 0], top[:, :, 1], top[:, :, 0], ALU.subtract).then_inc(S["power_in"], 1)
                else:
                    ps = bT[:, 0:GT * E1].rearrange("p (t e) -> p t e", e=E1)
                    ch.link(dve.tensor_scalar(lg[:, :, 0:E1], ps, -1.0 / WSCALE, None, ALU.mult))
                    dve.tensor_tensor(pin[:, :, :], lg[:, :, 0:E1], rb[:, :].unsqueeze(1).broadcast_to([P, GT, E1]),
                                      ALU.subtract).then_inc(S["power_in"], 1)

            def route_top(b, g, kind):
                wait(dve, "power_out", b["power_out"] + g + 1)
                wait(dve, "power_in", b["power_in"] + g + 1)
                if kind == "F0":
                    ch.link(dve.tensor_scalar(gw[:, :, 1], pout[:, :, 0], 1.0, None, ALU.add))
                    ch.link(dve.reciprocal(gw[:, :, 0], gw[:, :, 1]))
                    ch.link(dve.tensor_tensor(gw[:, :, 1], pout[:, :, 0], gw[:, :, 0], ALU.mult))
                else:
                    ch.link(dve.tensor_scalar(lg[:, :, 0:E1], pout[:, :, :], 1.0, None, ALU.add))
                    ch.link(dve.reciprocal(lg[:, :, 0:E1], lg[:, :, 0:E1]))
                    find_top(lg, E1)

            def route_gates(b, g, kind):
                n, ne, weight = (E0, E0, gw) if kind == "F0" else (E1, E1 + 1, top)
                for k in (0, 1):
                    ch.add(dve.tensor_tensor(eq[:, k, :, 0:n], experts[:, :, 0:n], topf[:, :, k:k + 1].broadcast_to([P, GT, n]),
                                             ALU.is_equal))
                ch.join()
                for k in (0, 1):
                    ch.add(dve.tensor_tensor(eq[:, k, :, 0:n], eq[:, k, :, 0:n], weight[:, :, k:k + 1].broadcast_to([P, GT, n]), ALU.mult))
                ch.join()
                ch.link(dve.tensor_tensor(gate[:, :, 0:n], eq[:, 0, :, 0:n], eq[:, 1, :, 0:n], ALU.add))
                wait(dve, "gatesT_ready", b["gatesT_ready"] + g)
                if kind == "F1":
                    ch.link(dve.memset(gate[:, :, E1:E1 + 1], 1.0))
                part = [gparts[:, :, k * ne:(k + 1) * ne] for k in range(3)]
                ch.link(dve.tensor_copy(part[0], gate[:, :, 0:ne]))
                ch.link(dve.tensor_tensor(gres[:, :, 0:ne], gate[:, :, 0:ne], part[0], ALU.subtract))
                ch.link(dve.tensor_copy(part[1], gres[:, :, 0:ne]))
                dve.tensor_tensor(part[2], gres[:, :, 0:ne], part[1], ALU.subtract).then_inc(S["gates_ready"], 1)

            def x_update(b, g):
                wait(dve, "outT_ready", b["outT_ready"] + g + 1)
                dst = x[:, bass.ts(g, GT), :]
                dve.tensor_tensor(dst, dst, bT[:, :].rearrange("p (t d) -> p t d", d=P), ALU.add).then_inc(S["x_updated"], 1)

            def layer(kind, b, per):
                nt = NT[kind]

                def group(g):
                    for j in range(nt):
                        t = nt * g + j
                        wait(dve, "silu_ready", b["silu_ready"] + t + 1)
                        wait(dve, "u_ready", b["u_ready"] + t + 1)
                        if j == 0:
                            wait(dve, "h_ready", b["h_ready"] + nt * g)
                        dve.tensor_tensor(m[:, j % 2, :], silu[:, j % 2, :], bU[j % 2][:, :], ALU.mult).then_inc(S["m_ready"], 1)
                        wait(dve, "m_ready", b["m_ready"] + t + 1)
                        wait(dve, "gx_ready", b["gx_ready"] + t + 1)
                        wait_slot(dve, "hlo_ready", b, nt, g, j, FRING)
                        dve.tensor_tensor(h[:, j % FRING, :], m[:, j % 2, :], bG[j % 2][:, :], ALU.mult).then_inc(S["h_ready"], 1)
                        if j == 3 and not is_first(g):
                            x_update(b, g - 1)
                        if b is base[0] and kind == "F0" and is_first(g) and j in W_AT:
                            w_lo(W_AT.index(j))
                        if not is_last(g):
                            if j == 0:
                                if b is base[0] and is_first(g):
                                    for i in range(1, NG):
                                        dve.wait_ge(x_loaded[i], 16)
                                ln_stats(b, g + 1)
                            if j == 1:
                                ln_apply(b, g + 1)
                            if j == 5:
                                x_lo(b, g + 1)
                            if j == 7:
                                route_begin(b, g + 1, kind)
                            if j == TOP_AT[kind]:
                                route_top(b, g + 1, kind)
                            if j == GATES_AT[kind]:
                                route_gates(b, g + 1, kind)
                wait(dve, "x_updated", b["x_updated"])
                if b["x_updated"] == 0:
                    dve.wait_ge(x_loaded[0], 16)
                ln_stats(b, 0)
                ln_apply(b, 0)
                x_lo(b, 0)
                route_begin(b, 0, kind)
                route_top(b, 0, kind)
                route_gates(b, 0, kind)
                groups(nc.vector, group, ch, per)
                x_update(b, NG - 1)

            def mamba(b):
                def prepare():
                    dve.wait_ge(mamba_loaded, ALL_MLOADS)
                    for n in range(2):
                        ch.add(dve.memset(xm[n][:, :, 0:PAD], 0.0))
                        ch.add(dve.tensor_scalar(w3g[:, n, :], w3[:, n, :], lng[:, n:n + 1], None, ALU.mult))
                    dve.tensor_copy(lnbw[:, :, :], lnb[:, :].unsqueeze(2).broadcast_to([P, 2, P])).then_inc(mprep_dve, 1)
                    for k in range(TAPS):
                        dve.wait_ge(wchi_ready, k + 1)
                        ch.add(dve.scalar_tensor_tensor(wc[1][:, k, :], [bA[0], bA[1], bU[0], bU[1]][k][:, 0:CH], CS, wc[0][:, k, :],
                                                        ALU.mult, ALU.subtract))
                    dve.wait_ge(wchi_ready, TAPS + 1)
                    ch.add(dve.scalar_tensor_tensor(wdts[:, 1, :], wdt[:, :], CS, wdts[:, 0, :], ALU.mult, ALU.subtract))
                    dve.wait_ge(mprep_act, 3)
                    ch.join()
                    dve.scalar_tensor_tensor(win2s[:, 1, :], win2[:, :], CS, win2s[:, 0, :], ALU.mult, ALU.subtract).then_inc(mprep_dve, 1)

                def g_mask(g):
                    for q in range(2):
                        wait(dve, "g_ready", b["g_ready"] + 2 * g + q + 1)
                        src = mG[q][:, 0:4 * P].rearrange("p (t c) -> p t c", t=2)[:, :, 0:P]
                        dve.tensor_tensor(gm[:, 2 * q:2 * q + 2, :], src, tri[:, :].unsqueeze(1).broadcast_to([P, 2, P]),
                                          ALU.mult).then_inc(S["gm_ready"], 1)

                def mixers(g):
                    wait(dve, "gm_ready", b["gm_ready"] + 2 * g + 2)
                    wait(dve, "yd_ready", b["yd_ready"] + 2 * g)
                    for t in range(GT):
                        wait(dve, "decay_ready", b["decay_ready"] + GT * g + t + 1)
                        dve.tensor_tensor(mt[:, t, :].rearrange("p (h l) -> p h l", l=P), decay[:, t, :].rearrange("p (h l) -> p h l", l=P),
                                          gm[:, t, :].unsqueeze(1).broadcast_to([P, HEADS, P]), ALU.mult).then_inc(S["mt_ready"], 1)

                def x_lo_pair(g):
                    wait(dve, "xhi_ready", b["xhi_ready"] + g + 1)
                    dve.tensor_tensor(pair(xm[1]), bT[:, :].rearrange("p (q s) -> p q s", q=2), pair(xm[0]),
                                      ALU.subtract).then_inc(S["xlo_ready"], 1)

                def dt_clip(g):
                    wait(dve, "dt_ready", b["dt_ready"] + g + 1)
                    src = bT[:, 0:GT * HEADS].rearrange("p (t h) -> p t h", t=GT)
                    ch.link(dve.tensor_scalar(dt[:, :, :], src, 1.0 / CS, None, ALU.mult))
                    ch.add(dve.tensor_scalar(dtx[:, :, :], dt[:, :, :], 20.0, 0.0, ALU.subtract, ALU.max))
                    dve.tensor_scalar(dtc[:, :, :], dt[:, :, :], 20.0, None, ALU.min).then_inc(S["dtc_ready"], 1)

                def dt_rate(g):
                    ch.join()
                    wait(dve, "sp_ready", b["sp_ready"] + g + 1)
                    ch.link(dve.tensor_tensor(dt[:, :, :], sp[:, :, :], dtx[:, :, :], ALU.add))
                    wait(dve, "cum_ready", b["cum_ready"] + g)
                    wait(dve, "trid_ready", b["trid_ready"] + GT * g)
                    dve.tensor_tensor(dd[:, :, :], dt[:, :, :], rate[:, :].unsqueeze(1).broadcast_to([P, GT, HEADS]),
                                      ALU.mult).then_inc(S["d_ready"], 1)

                def mix(g):
                    wait(dve, "yoff_ready", b["yoff_ready"] + g + 1)
                    wait(dve, "gelu_ready", b["gelu_ready"] + 2 * g + 2)
                    ch.link(dve.tensor_tensor(yo[:, :, :].rearrange("p q (h d) -> p q h d", d=HD),
                                              mY[:, :].rearrange("p (q h d) -> p q h d", q=2, h=HEADS),
                                              ed[:, 1, :, :].unsqueeze(3).broadcast_to([P, 2, HEADS, HD]), ALU.mult))
                    for q in range(2):
                        ch.add(dve.tensor_tensor(yo[:, q, :], mU[q][:, INNER:2 * INNER], yo[:, q, :], ALU.add))
                        ch.add(dve.tensor_tensor(hm[:, 2 * q, :], mU[q][:, 0:INNER], u2[:, 2 * q, :], ALU.mult))
                    ch.join()
                    odd = hm[:, :, :].rearrange("p (q t) c -> p q t c", t=2)[:, :, 1, :]
                    dve.tensor_tensor(odd, yo[:, :, :], u2[:, :, :].rearrange("p (q t) c -> p q t c", t=2)[:, :, 1, :],
                                      ALU.mult).then_inc(S["mixed"], 1)

                def hidden_norm(g):
                    wait(dve, "mixed", b["mixed"] + g + 1)
                    for t in range(GT):
                        ch.add(dve.bn_stats(hstats[:, t, :], hm[:, t, :]))
                    ch.join()
                    for t in range(GT):
                        ins = dve.bn_aggr(hmv[:, t, :], hstats[:, t, :])
                        if t < GT - 1:
                            ch.add(ins)
                        else:
                            ins.then_inc(S["hvar_ready"], 1)

                def hidden_apply(g):
                    ch.join()
                    wait(dve, "hrstd_ready", b["hrstd_ready"] + g + 1)
                    wait(dve, "hnT_ready", b["hnT_ready"] + 2 * g)
                    for t in range(GT):
                        ins = dve.tensor_scalar(hn[:, t, :], hm[:, t, :], hmv[:, t, 0:1], hrstd[:, t:t + 1], ALU.subtract, ALU.mult)
                        if t < GT - 1:
                            ch.add(ins)
                        else:
                            ins.then_inc(S["hn_ready"], 1)

                def prelu(dst, src, neg, name):
                    n = src.shape[0]
                    ch.link(dve.tensor_scalar(neg, src, 0.0, slope[0:n, 0:1], ALU.min, ALU.mult))
                    dve.scalar_tensor_tensor(dst, src, 0.0, neg, ALU.max, ALU.add).then_inc(S[name], 1)

                def x_conv(g):
                    for n in range(2):
                        wait(dve, "convx_ready", b["convx_ready"] + 2 * g + n + 1)
                        dve.scalar_tensor_tensor(xc[:, 2 * n:2 * n + 2, :], mX[n][:, :].rearrange("p (t c) -> p t c", t=2), 1.0 / CS,
                                                 xbias[:, :].unsqueeze(1).broadcast_to([P, 2, INNER]), ALU.mult, ALU.add)\
                           .then_inc(S["xc_biased"], 1)
                    wait(dve, "xc_biased", b["xc_biased"] + 2 * g + 2)
                    wait(dve, "yd_ready", b["yd_ready"] + 2 * g)
                    wait(dve, "xs_ready", b["xs_ready"] + g)
                    prelu(xv[:, :, :].rearrange("p t c -> p (t c)"), xc[:, :, :].rearrange("p t c -> p (t c)"),
                          xneg[:, :, :].rearrange("p t c -> p (t c)"), "xs_val")

                def bc_conv(g):
                    for n in range(2):
                        wait(dve, "bc_biased", b["bc_biased"] + 2 * g + n + 1)
                        wait(dve, "g_ready", b["g_ready"] + 2 * g)
                        prelu(bcv[:, n, :], bcc[:, n, :], bcneg[:, n, :], "bc_val")

                def hnT_copy(g):
                    wait(dve, "hnT_ready", b["hnT_ready"] + 2 * g + 2)
                    wait(dve, "y_ready", b["y_ready"] + g)
                    dve.tensor_copy(hnT[:, 1, :], bT[:, :]).then_inc(S["hnT1_copied"], 1)

                def x_update(g):
                    wait(dve, "y_ready", b["y_ready"] + g + 1)
                    wait(dve, "x_biased", b["x_biased"] + g + 1)
                    dst = x[:, bass.ts(g, GT), :]
                    dve.tensor_tensor(dst, dst, mY[:, :].rearrange("p (t d) -> p t d", d=P), ALU.add).then_inc(S["x_updated"], 1)

                def body(g):
                    nxt = not is_last(g)
                    if nxt:
                        ln_stats(b, g + 1)
                        ln_apply(b, g + 1)
                    g_mask(g)
                    mixers(g)
                    if nxt:
                        x_lo_pair(g + 1)
                        dt_clip(g + 1)
                    mix(g)
                    hidden_norm(g)
                    if nxt:
                        dt_rate(g + 1)
                    hidden_apply(g)
                    if nxt:
                        x_conv(g + 1)
                        bc_conv(g + 1)
                    hnT_copy(g)
                    x_update(g)
                prepare()
                if b["x_updated"] == 0:
                    for g in range(NG):
                        dve.wait_ge(x_loaded[g], 16)
                wait(dve, "x_updated", b["x_updated"])
                ln_stats(b, 0)
                ln_apply(b, 0)
                x_lo_pair(0)
                dt_clip(0)
                dt_rate(0)
                x_conv(0)
                bc_conv(0)
                with nc.vector.Fori(0, NG - 1) as g:
                    body(g)
                body(NG - 1)

            def attention(b):
                def prepare():
                    dve.wait_ge(aprep_act, 2)
                    dve.scalar_tensor_tensor(wqks[:, 1, :], wqk[:, :], WSCALE, wqks[:, 0, :], ALU.mult, ALU.subtract).then_inc(aprep_dve, 1)
                    dve.scalar_tensor_tensor(wvs[:, 1, :], wv[:, :], WSCALE, wvs[:, 0, :], ALU.mult, ALU.subtract).then_inc(aprep_dve, 1)
                    for part in range(2):
                        for a in range(2):
                            ones = va[:, a, :, part, :].rearrange("p t (h e) -> p t h e", e=AD + 1)[:, :, :, AD:AD + 1]
                            ins = dve.memset(ones, 1.0 - part)
                    ins.then_inc(aprep_dve, 1)

                def x_lo(q):
                    wait(dve, "xhi_ready", b["xhi_ready"] + q.value + 1)
                    cols = slice(q.parity * SEQ, (q.parity + 1) * SEQ)
                    dve.tensor_tensor(xa[1][:, cols], bT[:, 0:SEQ], xa[0][:, cols], ALU.subtract).then_inc(S["xlo_ready"], 1)

                def rope_mul(q):
                    wait(dve, "qk_ready", b["qk_ready"] + q.value + 1)
                    if q.index >= 1:
                        wait(dve, "roped", b["roped"] + q.value)
                    src = sets[0][:, :].rearrange("p (n k s) -> p n k s", n=2, k=2)
                    for k, table in enumerate((ropec, ropes)):
                        ins = dve.scalar_tensor_tensor(rope[:, :, k, :], src[:, :, k, :], 1.0 / WSCALE,
                                                       table[:, :].unsqueeze(1).broadcast_to([P, 2, SEQ]), ALU.mult, ALU.mult)
                    ins.then_inc(S["rope_mul"], 1)

                def v_lo(q):
                    wait(dve, "v_copied", b["v_copied"] + q.value + 1)
                    for t in range(2):
                        hi, lo = (va[:, q.parity, t, part, :].rearrange("p (h e) -> p h e", e=AD + 1)[:, :, 0:AD] for part in range(2))
                        ins = dve.scalar_tensor_tensor(lo, sets[1][:, t * P:(t + 1) * P].rearrange("p (h e) -> p h e", e=AD),
                                                       1.0 / WSCALE, hi, ALU.mult, ALU.subtract)
                    ins.then_inc(S["vlo_ready"], 1)

                def unit_max(q, u):
                    wait(dve, "s1_ready", b["s1_ready"] + NU * q.value + u + 1)
                    qt, kt = UNITS[u // 2]
                    src = sets[2 * u % 3][:, :].rearrange("p (h k) -> p h k", k=P)
                    if qt == kt:
                        ch.link(dve.tensor_tensor(masked[:, u % 2, :, :], src, maskq[:, :].unsqueeze(1).broadcast_to([P, 8, P]), ALU.add))
                        src = masked[:, u % 2, :, :]
                    dve.tensor_reduce(mx[:, u // 2, (u % 2) * 8:(u % 2) * 8 + 8], src, AX, ALU.max).then_inc(S["max_ready"], 1)

                def negate(q):
                    wait(dve, "max_ready", b["max_ready"] + NU * q.value + NU)
                    ch.link(dve.tensor_tensor(mx[:, 1, :], mx[:, 1, :], mx[:, 2, :], ALU.max))
                    ch.link(dve.tensor_scalar(negm[:, :, :], mx[:, 0:2, :], -1.0, None, ALU.mult))
                    wait(dve, "mT_ready", b["mT_ready"] + q.value)
                    ch.link(dve.tensor_copy(mparts[:, :, 0:AH], negm[:, :, :]))
                    dve.tensor_tensor(mparts[:, :, AH:2 * AH], negm[:, :, :], mparts[:, :, 0:AH], ALU.subtract).then_inc(S["negmax"], 1)

                def normalise(q):
                    wait(dve, "pv_done", b["pv_done"] + NU * (q.value + 1))
                    o = bO[:, 0:2 * AH * (AD + 1)].rearrange("p (t h e) -> p t h e", t=2, e=AD + 1)
                    ch.link(dve.reciprocal(orec[:, :, :], o[:, :, :, AD]))
                    wait(dve, "oTa_ready", b["oTa_ready"] + q.value)
                    dve.tensor_tensor(on[:, :, :].rearrange("p t (h e) -> p t h e", e=AD), o[:, :, :, 0:AD],
                                      orec[:, :, :].unsqueeze(3).broadcast_to([P, 2, AH, AD]), ALU.mult).then_inc(S["onorm"], 1)

                def x_update(q):
                    wait(dve, "ya_ready", b["ya_ready"] + q.value + 1)
                    wait(dve, "x_biased", b["x_biased"] + q.half + 1)
                    dst = x[:, bass.ts(q.value, 2), :]
                    dve.tensor_tensor(dst, dst, bT[:, SEQ:2 * SEQ].rearrange("p (t d) -> p t d", d=P), ALU.add).then_inc(S["x_updated"], 1)

                def step(q):
                    if q.index < NSEQ - 3 and q.parity == 1:
                        ln_stats(b, q.half + 2)
                        ln_apply(b, q.half + 2, 2)
                    for u in range(NU):
                        if q.index < NSEQ - 1:
                            unit_max(q.plus(1), u)
                        if u == 1 and q.index:
                            x_update(q.plus(-1))
                        if u == 4 and q.index < NSEQ - 3:
                            x_lo(q.plus(3))
                    if q.index < NSEQ - 1:
                        negate(q.plus(1))
                    if q.index < NSEQ - 3:
                        rope_mul(q.plus(3))
                    normalise(q)
                    if q.index < NSEQ - 2:
                        v_lo(q.plus(2))
                if b["x_updated"] == 0:
                    for g in range(NG):
                        dve.wait_ge(x_loaded[g], 16)
                wait(dve, "x_updated", b["x_updated"])
                prepare()
                ln_stats(b, 0)
                ln_apply(b, 0, 2)
                for q in (Seq(0), Seq(1)):
                    x_lo(q)
                    rope_mul(q)
                ln_stats(b, 1)
                ln_apply(b, 1, 2)
                for q in (Seq(0), Seq(1)):
                    v_lo(q)
                x_lo(Seq(2))
                rope_mul(Seq(2))
                for u in range(NU):
                    unit_max(Seq(0), u)
                negate(Seq(0))
                steps(nc.vector, step)
                x_update(Seq(NSEQ - 1))
            dve.wait_ge(consts_loaded, ALL_CONSTS)
            for ph, b in zip(phases, base):
                {"M": mamba, "A": attention}[ph](b) if ph in "MA" else layer(ph, b, {"F0": 31, "F1": 31}[ph])

        @block.tensor
        def _(pe):
            def split_product(out, w, wcols, rhs_hi, rhs_lo, start=True, stop=True):
                nc.tensor.matmul(out, w[0][:, wcols], rhs_hi, start=start, stop=False)
                nc.tensor.matmul(out, w[0][:, wcols], rhs_lo, start=False, stop=False)
                return nc.tensor.matmul(out, w[1][:, wcols], rhs_hi, start=False, stop=stop)

            def xn_transpose(b, g):
                wait(pe, "xn_ready", b["xn_ready"] + g + 1)
                for i in range(GT):
                    ins = nc.tensor.transpose(bT[:, i * P:(i + 1) * P], xn[:, i, :], ident[:, :])
                ins.then_inc(S["xnT_ready"], 1)

            def logits(b, g, k):
                n = (E0, E1)[k]
                wait(pe, "xlo_ready", b["xlo_ready"] + g + 1)
                for i in range(GT):
                    tok = bass.ds(g * GROUP + i * P, P)
                    o = bT[:, i * n:(i + 1) * n]
                    nc.tensor.matmul(o, xhi[:, tok], wrs[k][:, 0, :], start=i == 0, stop=False, skip_group_check=True)
                    nc.tensor.matmul(o, xhi[:, tok], wrs[k][:, 1, :], start=False, stop=False, skip_group_check=True)
                    ins = nc.tensor.matmul(o, xlo[:, tok], wrs[k][:, 0, :], start=False, stop=True, skip_group_check=True)
                ins.then_inc(S["logits_ready"], 1)

            def gates_transpose(b, g, kg):
                wait_apart(pe, "gates_ready", b["gates_ready"] + g + 1)
                for i in range(GT):
                    ins = nc.tensor.transpose(bTb[:, i * P:(i + 1) * P], gparts[:, i, :], identb[:, :])
                ins.then_inc(S["gatesT_ready"], 1)

            def out_transpose(b, g):
                wait(pe, "o_copied", b["o_copied"] + g + 1)
                for i in range(GT):
                    ins = nc.tensor.transpose(bT[:, i * P:(i + 1) * P], oT[:, i * P:(i + 1) * P], ident[:, :])
                ins.then_inc(S["outT_ready"], 1)

            def layer(kind, b):
                k = 0 if kind == "F0" else 1
                nt, kg = NT[kind], 3 * (E0 if k == 0 else E1 + 1)

                def up(g, j):
                    cols = slice(j * P, (j + 1) * P)
                    hi, lo = xhi[:, bass.ts(g, GROUP)], xlo[:, bass.ts(g, GROUP)]
                    wait_slot(pe, "silu_ready", b, nt, g, j, 2)
                    split_product(bA[j % 2][:, :], W["w1g", k], cols, hi, lo).then_inc(S["a_ready"], 1)
                    wait_slot(pe, "m_ready", b, nt, g, j, 2)
                    split_product(bU[j % 2][:, :], W["w1u", k], cols, hi, lo).then_inc(S["u_ready"], 1)

                def gates(g, j):
                    cols = slice(j * P, (j + 1) * P)
                    wait_slot(pe, "h_ready", b, nt, g, j, 2)
                    if j == 0:
                        wait(pe, "gT_ready", b["gT_ready"] + g + 1)
                    nc.tensor.matmul(bG[j % 2][:, :], sel[k][:, cols], gT[:, bass.ts(g, GROUP)],
                                     start=True, stop=True).then_inc(S["gx_ready"], 1)

                def down(g, j):
                    r = j % HRING
                    wait(pe, "hlo_ready", b["hlo_ready"] + nt * g + j + 1)
                    if j == 0:
                        wait(pe, "o_copied", b["o_copied"] + g)
                    split_product(bO[:, :], W["w2", k], slice(j * P, (j + 1) * P), hhi[:, r, :], hlo[:, r, :],
                                  start=j == 0, stop=j == nt - 1).then_inc(S["h_used"], 1)

                def group(g):
                    for j in range(nt):
                        if not (is_first(g) and j == 1):
                            up(g, j)
                        if is_first(g) and j == 0:
                            up(g, 1)
                            gates_transpose(b, 0, kg)
                        gates(g, j)
                        if j >= LAG:
                            down(g, j - LAG)
                        elif not is_first(g):
                            down(g - 1, nt + j - LAG)
                        if j == 3 and not is_first(g):
                            out_transpose(b, g - 1)
                        if not is_last(g):
                            if j == 4:
                                if not is_first(g):
                                    wait(pe, "x_updated", b["x_updated"] + g)
                                xn_transpose(b, g + 1)
                            if j == 6:
                                logits(b, g + 1, k)
                            if j == GATES_T_AT[kind]:
                                gates_transpose(b, g + 1, kg)
                if k == 1:
                    pe.wait_ge(wlo_ready, ALL_WEIGHTS)
                xn_transpose(b, 0)
                logits(b, 0, k)
                groups(nc.tensor, group)
                for j in range(nt - LAG, nt):
                    down(NG - 1, j)
                out_transpose(b, NG - 1)
            pe.wait_ge(consts_loaded, ALL_CONSTS)
            pe.wait_ge(idents_loaded, 32)
            pe.wait_ge(wlo_ready, EARLY)

            def mamba(b):
                def prepare():
                    pe.wait_ge(mamba_loaded, ALL_MLOADS)
                    wait(pe, "x_updated", b["x_updated"])
                    for k in range(TAPS):
                        for c in range(CH // P):
                            ins = nc.tensor.matmul([bA[0], bA[1], bU[0], bU[1]][k][:, 0:CH], win1[:, c, :], convw[:, c, k, :],
                                                   start=c == 0, stop=c == CH // P - 1)
                        ins.then_inc(wc_ready, 1)
                    pe.wait_ge(mprep_dve, 1)
                    for k in range(2):
                        ins = nc.tensor.matmul(bT[:, 0:P], lnbw[:, k, :], w3[:, k, :], start=k == 0, stop=k == 1)
                    ins.then_inc(wc_ready, 1)
                    pe.wait_ge(mprep_act, 2)
                    pe.wait_ge(mprep_dve, 2)

                def taps(out, lhs, rhs):
                    for k in range(TAPS):
                        for n, (p, q) in enumerate(((0, 0), (0, 1), (1, 0))):
                            ins = nc.tensor.matmul(out, lhs(p, k), rhs(q, k), start=k == 0 and n == 0, stop=k == TAPS - 1 and n == 2)
                    return ins

                def tile_of(part, t, k):
                    at = PAD - (TAPS - 1) + k + (t % 2) * P
                    return xm[part][:, t // 2, at:at + P]

                def seg(g):
                    wait(pe, "gelu_ready", b["gelu_ready"] + 2 * g + 2)
                    wait(pe, "bc_biased", b["bc_biased"] + 2 * g + 2)
                    for t in range(GT):
                        wait(pe, "trid_ready", b["trid_ready"] + GT * g + t + 1)
                        nc.tensor.matmul(mSeg[t][:, :], later[:, :], trid[:, t, :], start=True, stop=True).then_inc(S["seg_ready"], 1)
                    wait(pe, "x_updated", b["x_updated"] + g)
                    for n, m_ in ((0, later), (1, tri)):
                        ins = nc.tensor.matmul(mCum[:, n * 2 * HEADS:(n + 1) * 2 * HEADS].rearrange("p (q h) -> p q h", q=2), m_[:, :],
                                               dd[:, :, :].rearrange("p (q t) h -> p q t h", t=2)[:, :, n, :],
                                               start=n == 0, stop=True, skip_group_check=True)
                    ins.then_inc(S["cum_ready"], 1)

                def g_blocks(g):
                    wait(pe, "bc_val", b["bc_val"] + 2 * g + 2)
                    wait(pe, "xc_biased", b["xc_biased"] + 2 * g + 2)
                    for q in range(2):
                        o = q * SEQ
                        nc.tensor.matmul(mG[q][:, 0:SEQ], bcv[:, 0, o:o + P], bcv[:, 1, o:o + SEQ], start=True, stop=True)
                        nc.tensor.matmul(mG[q][:, SEQ:SEQ + P], bcv[:, 0, o + P:o + SEQ], bcv[:, 1, o + P:o + SEQ],
                                         start=True, stop=True).then_inc(S["g_ready"], 1)

                def dt_project(g):
                    wait(pe, "xlo_ready", b["xlo_ready"] + g + 1)
                    for t in range(GT):
                        o = bT[:, t * HEADS:(t + 1) * HEADS]
                        for n, (p, q) in enumerate(((0, 0), (0, 1), (1, 0))):
                            ins = nc.tensor.matmul(o, tile_of(p, t, TAPS - 1), wdts[:, q, :], start=t == 0 and n == 0, stop=n == 2,
                                                   skip_group_check=True)
                    ins.then_inc(S["dt_ready"], 1)

                def y_products(g):
                    wait(pe, "xs_val", b["xs_val"] + g + 1)
                    for t in range(GT):
                        wait(pe, "mt_ready", b["mt_ready"] + GT * g + t + 1)
                        for hd in range(HEADS):
                            o = (t % 2) * INNER + hd * HD
                            ins = nc.tensor.matmul(mU[t // 2][:, o:o + HD], mt[:, t, hd * P:(hd + 1) * P], xv[:, t, hd * HD:(hd + 1) * HD],
                                                   start=True, stop=True)
                        if t % 2:
                            ins.then_inc(S["yd_ready"], 1)
                    wait(pe, "goff_ready", b["goff_ready"] + 2 * g + 2)
                    wait(pe, "xs_ready", b["xs_ready"] + g + 1)
                    for q in range(2):
                        ins = nc.tensor.matmul(mY[:, q * INNER:(q + 1) * INNER], goff[:, q, :], xsd[:, q, :], start=True, stop=True)
                    ins.then_inc(S["yoff_ready"], 1)

                def convolve(g):
                    wait(pe, "goff_ready", b["goff_ready"] + 2 * g)
                    for n in range(2):
                        for t in (2 * n, 2 * n + 1):
                            ins = taps(mX[n][:, (t % 2) * INNER:(t % 2 + 1) * INNER], lambda p, k: tile_of(p, t, k),
                                       lambda q, k: wc[q][:, k, 0:INNER])
                        ins.then_inc(S["convx_ready"], 1)
                    wait(pe, "decay_ready", b["decay_ready"] + GT * g)
                    for n, (bk, s) in enumerate(((mB, "convb_ready"), (mC, "convc_ready"))):
                        c = INNER + n * STATE
                        taps(bk[0:STATE, :].rearrange("p (q s) -> p q s", q=2), lambda p, k: wc[p][:, k, c:c + STATE],
                             lambda q, k: xm[q][:, :, PAD - (TAPS - 1) + k:PAD - (TAPS - 1) + k + SEQ]).then_inc(S[s], 1)
                    wait(pe, "mixed", b["mixed"] + g)
                    for t in range(GT):
                        for n, (p, q) in enumerate(((0, 0), (0, 1), (1, 0))):
                            ins = nc.tensor.matmul(mU[t // 2][:, (t % 2) * INNER:(t % 2 + 1) * INNER], tile_of(p, t, TAPS - 1), win2s[:, q, :],
                                                   start=n == 0, stop=n == 2)
                        if t % 2:
                            ins.then_inc(S["u2_ready"], 1)

                def out_product(g):
                    wait(pe, "hn_ready", b["hn_ready"] + g + 1)
                    if not is_last(g):
                        wait(pe, "dtc_ready", b["dtc_ready"] + g + 2)
                    for k, bk in enumerate((mY, bT)):
                        for t in range(GT):
                            ins = nc.tensor.transpose(bk[:, t * P:(t + 1) * P], hn[:, t, k * P:(k + 1) * P], ident[:, :])
                        ins.then_inc(S["hnT_ready"], 1)
                    wait(pe, "hnT0_copied", b["hnT0_copied"] + g + 1)
                    wait(pe, "hnT1_copied", b["hnT1_copied"] + g + 1)
                    for t in range(GT):
                        for k in range(2):
                            ins = nc.tensor.matmul(mY[:, t * P:(t + 1) * P], hnT[:, k, t * P:(t + 1) * P], w3g[:, k, :],
                                                   start=k == 0, stop=k == 1)
                    ins.then_inc(S["y_ready"], 1)

                def body(g):
                    nxt = not is_last(g)
                    seg(g)
                    g_blocks(g)
                    if nxt:
                        wait(pe, "hnT1_copied", b["hnT1_copied"] + g)
                        xn_transpose(b, g + 1)
                        dt_project(g + 1)
                    y_products(g)
                    if nxt:
                        convolve(g + 1)
                    out_product(g)
                prepare()
                xn_transpose(b, 0)
                dt_project(0)
                convolve(0)
                with nc.tensor.Fori(0, NG - 1) as g:
                    body(g)
                body(NG - 1)

            def attention(b):
                def tokens_transpose(q):
                    wait(pe, "xn_ready", b["xn_ready"] + q.half + 1)
                    for t in range(2):
                        ins = nc.tensor.transpose(bT[:, t * P:(t + 1) * P], xn[:, 2 * q.parity + t, :], ident[:, :])
                    ins.then_inc(S["xnT_ready"], 1)

                def project(q):
                    cols = slice(q.parity * SEQ, (q.parity + 1) * SEQ)
                    wait(pe, "xlo_ready", b["xlo_ready"] + q.value + 1)
                    for n in range(4):
                        c, o = slice(n * P, (n + 1) * P), sets[0][:, n * SEQ:(n + 1) * SEQ]
                        nc.tensor.matmul(o, wqks[:, 0, c], xa[0][:, cols], start=True, stop=False)
                        nc.tensor.matmul(o, wqks[:, 0, c], xa[1][:, cols], start=False, stop=False)
                        ins = nc.tensor.matmul(o, wqks[:, 1, c], xa[0][:, cols], start=False, stop=True)
                    ins.then_inc(S["qk_ready"], 1)

                def values(q):
                    for t in range(2):
                        cols = slice(q.parity * SEQ + t * P, q.parity * SEQ + (t + 1) * P)
                        o = sets[1][:, t * P:(t + 1) * P]
                        nc.tensor.matmul(o, xa[0][:, cols], wvs[:, 0, :], start=True, stop=False)
                        nc.tensor.matmul(o, xa[1][:, cols], wvs[:, 0, :], start=False, stop=False)
                        ins = nc.tensor.matmul(o, xa[0][:, cols], wvs[:, 1, :], start=False, stop=True)
                    ins.then_inc(S["v_ready"], 1)

                def scores(dst, u, mask, lhs, rhs, rows, name):
                    qt, kt = UNITS[u // 2]
                    for ii in range(2):
                        if mask is not None and qt == kt:
                            nc.tensor.matmul(dst[:, ii * 512:(ii + 1) * 512], identb[:, :], mask[:, :], start=True, stop=False,
                                             skip_group_check=True)
                    for j in range(4):
                        for ii in range(2):
                            r = 32 * (2 * (u % 2) + ii)
                            ins = nc.tensor.matmul(dst[:, (4 * ii + j) * P:(4 * ii + j + 1) * P],
                                                   lhs[0][r:r + rows, j, lhs[1] * P:(lhs[1] + 1) * P],
                                                   rhs[0][r:r + rows, j, rhs[1] * P:(rhs[1] + 1) * P],
                                                   start=mask is None or qt != kt, stop=True, skip_group_check=True)
                    ins.then_inc(S[name], 1)

                def first_pass(q, u):
                    qt, kt = UNITS[u // 2]
                    if u == 0:
                        pe.wait_ge(spread_done[q.parity], SPREAD * (q.half + 1))
                    scores(sets[2 * u % 3], u, None, (qa[q.parity], qt), (ka[q.parity], kt), ROWS, "s1_ready")

                def second_pass(q, u):
                    qt, kt = UNITS[u // 2]
                    if u == 0:
                        pe.wait_ge(maxima_done, MAXIMA * (q.value + 1))
                    scores(sets[(2 * u + 1) % 3], u, maskk, (ka[q.parity], kt), (qa[q.parity], qt), 32, "s2_ready")

                def weighted(q, u):
                    qt, kt = UNITS[u // 2]
                    wait(pe, "plo_ready", b["plo_ready"] + NU * q.value + u + 1)
                    if u == 0:
                        wait(pe, "onorm", b["onorm"] + q.value)
                        wait(pe, "vlo_ready", b["vlo_ready"] + q.value + 1)
                    w = AD + 1
                    for hh in range(8):
                        hd = 8 * (u % 2) + hh
                        o = bO[:, (qt * AH + hd) * w:(qt * AH + hd + 1) * w]
                        hi, lo = (p[:, u % PRING, hh * P:(hh + 1) * P] for p in (phi, plo))
                        v_hi, v_lo = (va[:, q.parity, kt, part, hd * w:(hd + 1) * w] for part in range(2))
                        nc.tensor.matmul(o, hi, v_hi, start=u == 0 and hh == 0, stop=False, skip_group_check=True)
                        nc.tensor.matmul(o, hi, v_lo, start=False, stop=False, skip_group_check=True)
                        ins = nc.tensor.matmul(o, lo, v_hi, start=False, stop=True, skip_group_check=True)
                    ins.then_inc(S["pv_done"], 1)

                def maxima_transpose(q):
                    wait_apart(pe, "negmax", b["negmax"] + q.value + 1)
                    for j in range(4):
                        for t in range(2):
                            ins = nc.tensor.transpose(mTh[0:8, (2 * j + t) * P:(2 * j + t + 1) * P], mparts[:, t, j::4], identh[:, :])
                    ins.then_inc(S["mT_ready"], 1)

                def heads_transpose(q):
                    wait(pe, "onorm", b["onorm"] + q.value + 1)
                    for t in range(2):
                        ins = nc.tensor.transpose(bT[:, t * P:(t + 1) * P], on[:, t, :], ident[:, :])
                    ins.then_inc(S["oTa_ready"], 1)

                def out_product(q):
                    wait(pe, "oTa_copied", b["oTa_copied"] + q.value + 1)
                    for t in range(2):
                        ins = nc.tensor.matmul(bT[:, SEQ + t * P:SEQ + (t + 1) * P], oTa[:, t * P:(t + 1) * P], wo[:, :], start=True, stop=True)
                    ins.then_inc(S["ya_ready"], 1)

                def step(q):
                    last = q.index == NSEQ - 1
                    for u in range(NU):
                        if not last:
                            if u == 0 and q.index < NSEQ - 2:
                                wait(pe, "rope_mul", b["rope_mul"] + q.value + 3)
                            if u >= 2:
                                wait(pe, "exp_ready", b["exp_ready"] + NU * q.value + u - 1)
                            first_pass(q.plus(1), u)
                        if q.index:
                            if u == 0:
                                heads_transpose(q.plus(-1))
                            if u == 1:
                                out_product(q.plus(-1))
                        if not last:
                            if u == 0:
                                wait(pe, "vlo_ready", b["vlo_ready"] + q.value + 2)
                            else:
                                wait(pe, "max_ready", b["max_ready"] + NU * (q.value + 1) + u)
                        elif u >= 3:
                            wait(pe, "exp_ready", b["exp_ready"] + NU * q.value + u - 2)
                        second_pass(q, u)
                        if u >= 2:
                            weighted(q, u - 2)
                        if u == 3 and q.index < NSEQ - 3:
                            wait(pe, "x_updated", b["x_updated"] + q.value)
                            tokens_transpose(q.plus(3))
                    weighted(q, NU - 2)
                    if q.index < NSEQ - 3:
                        wait(pe, "exp_ready", b["exp_ready"] + NU * q.value + NU - 1)
                        project(q.plus(3))
                    if not last:
                        maxima_transpose(q.plus(1))
                    weighted(q, NU - 1)
                    if q.index < NSEQ - 2:
                        values(q.plus(2))
                wait(pe, "x_updated", b["x_updated"])
                pe.wait_ge(aprep_dve, 3)
                for n in range(2):
                    wait(pe, "xlo_ready", b["xlo_ready"] + n)
                    tokens_transpose(Seq(n))
                    wait(pe, "rope_mul", b["rope_mul"] + n)
                    project(Seq(n))
                for n in range(2):
                    wait(pe, "vlo_ready", b["vlo_ready"] + n)
                    values(Seq(n))
                tokens_transpose(Seq(2))
                wait(pe, "rope_mul", b["rope_mul"] + 2)
                project(Seq(2))
                for u in range(NU):
                    if u == 0:
                        wait(pe, "rope_mul", b["rope_mul"] + 3)
                    if u == 2:
                        wait(pe, "vlo_ready", b["vlo_ready"] + 2)
                    if u > 2:
                        wait(pe, "max_ready", b["max_ready"] + u - 2)
                    first_pass(Seq(0), u)
                maxima_transpose(Seq(0))
                steps(nc.tensor, step)
                heads_transpose(Seq(NSEQ - 1))
                out_product(Seq(NSEQ - 1))
            for ph, b in zip(phases, base):
                {"M": mamba, "A": attention}[ph](b) if ph in "MA" else layer(ph, b)


_CONSTS = {}


LAYERS = ("F0", "M", "F0", "F1", "A", "F1")


def kernel(**inputs):
    import numpy as np
    import ml_dtypes
    import concourse.bacc as _bacc
    from concourse.bass_utils import run_bass_kernel_spmd as _run

    def cat(*a):
        return np.concatenate(a, axis=0)

    a = {k: np.asarray(v) for k, v in inputs.items()}
    experts_in = lambda w, s: cat(a[w], a[s][None])
    cols = lambda w: np.transpose(w.reshape(-1, w.shape[-1]), (1, 0))
    rows = lambda w: np.transpose(w.reshape(-1, P, P), (1, 0, 2)).reshape(P, -1)
    arrays = {
        "x": a["L0_attn_u"],
        "w1g0": np.transpose(a["L0_ffn_W1"], (1, 0, 2)).reshape(P, -1),
        "w1u0": np.transpose(a["L0_ffn_W3"], (1, 0, 2)).reshape(P, -1),
        "w20": rows(a["L0_ffn_W2"]),
        "w1g1": cols(experts_in("L1_ffn_Wg", "L1_ffn_Wg_s")),
        "w1u1": cols(experts_in("L1_ffn_Wu", "L1_ffn_Wu_s")),
        "w21": rows(np.transpose(experts_in("L1_ffn_Wd", "L1_ffn_Wd_s"), (0, 2, 1))),
        "wr0": a["L0_ffn_Wg"].T, "wr1": a["L1_ffn_Wr"].T, "rb": a["L1_ffn_rb"],
    }
    bf = ml_dtypes.bfloat16
    w_in, conv = a["L0_attn_W_in1"], a["L0_attn_conv_w"]
    taps_in = np.transpose(conv, (1, 2, 0)).reshape(CH // P, P, TAPS, CH)
    arrays.update({
        "win1": np.transpose(w_in[INNER:INNER + CH].reshape(CH // P, P, P), (1, 0, 2)),
        "convw": np.transpose(taps_in, (1, 0, 2, 3)),
        "wdt": w_in[INNER + CH:].T, "win2": a["L0_attn_W_in2"].T,
        "w3": np.transpose(a["L0_attn_W_in3"].T.reshape(2, P, P), (1, 0, 2)),
        "lng": a["L0_attn_ln_g"].reshape(2, P).T, "lnb": a["L0_attn_ln_b"].reshape(2, P).T,
        "xbias": a["L0_attn_conv_b"][:INNER], "bcbias": a["L0_attn_conv_b"][INNER:].reshape(2, STATE).T,
        "slope": a["L0_attn_prelu_a"].reshape(1), "alog": a["L0_attn_A_log"],
    })
    partner = np.roll(np.arange(P), P // 2)
    order = np.arange(P).reshape(AH, AD).T.reshape(P)
    wq, wk = a["L1_attn_wq"], a["L1_attn_wk"]
    arrays.update({"wqk": np.transpose(cat(wq[order], wq[partner[order]], wk[order], wk[partner[order]])), "wv": a["L1_attn_wv"].T,
                   "wo": a["L1_attn_out_w"].T, "obias": a["L1_attn_out_b"]})
    half = P // 2
    freqs = np.float32(1.0) / np.float32(10000.0) ** (np.arange(half, dtype=np.float32) / np.float32(half))
    ang = np.arange(SEQ, dtype=np.float32)[None, :] * freqs[:, None].astype(np.float32)
    arrays["ropec"] = np.tile(np.cos(ang), (2, 1))[order].astype(np.float32)
    arrays["ropes"] = cat(-np.sin(ang), np.sin(ang))[order].astype(np.float32)
    slopes = 2.0 ** (-8.0 * (np.arange(AH) + 1) / AH) * AD ** 0.5
    pos = np.arange(SEQ, dtype=np.float64)
    qinit, kinit = np.zeros((4, 32, 4, SEQ), np.float16), np.zeros((4, 32, 4, SEQ), np.float16)
    for n, v in enumerate((slopes[:, None] + 0 * pos, -slopes[:, None] * pos)):
        for k in range(3):
            part = v.astype(np.float16)
            v = v - part.astype(np.float64)
            qinit[:, 24 + 3 * n + k] = part.reshape(4, 4, SEQ)
    kinit[:, 24:27], kinit[:, 27:32] = pos, 1.0
    arrays["qinit"], arrays["kinit"] = qinit.reshape(P, 4, SEQ), kinit.reshape(P, 4, SEQ)
    future = np.triu(np.ones((P, P)), 1) * -4e9
    arrays["maskq"], arrays["maskk"] = future.astype(bf), np.tile(future.T, (1, 4)).astype(bf)
    arrays["identh"] = np.eye(P, dtype=np.float16)
    arrays["tri"] = np.triu(np.ones((P, P), np.float32))
    arrays["later"] = np.tril(np.ones((P, P), np.float32), -1)
    bf = ml_dtypes.bfloat16
    arrays["ident"] = np.eye(P, dtype=np.float32)
    arrays["identb"] = np.eye(P).astype(bf)
    arrays["experts"] = np.broadcast_to(np.arange(E0, dtype=np.float32), (P, GT, E0))
    for name, e, i in (("sel0", E0, I0), ("sel1", E1 + 1, I1)):
        s = np.tile(np.repeat(np.eye(e), i, axis=1), (3, 1))
        arrays[name] = cat(s, np.zeros((P - 3 * e, e * i))).astype(bf)

    nc = _bacc.Bacc("TRN2", target_bir_lowering=False, num_devices=1)
    io, feed = {}, {}
    for name, v in arrays.items():
        feed[name + "_dram"] = np.ascontiguousarray(v)
        io[name] = nc.dram_tensor(name + "_dram", v.shape, mybir.dt.from_np(v.dtype), kind="ExternalInput").ap()
    io["out"] = nc.dram_tensor("out_dram", a["L0_attn_u"].shape, F32, kind="ExternalOutput").ap()
    build(nc, io, LAYERS)
    r = _run(nc, [feed], core_ids=[0])
    return r.results[0]["out_dram"]
```
